# Optimizing a Trainium2 kernel written in Bass

```python
import numpy as np
import jax
import jax.numpy as jnp

def _softmax(x, axis=-1):
    return jax.nn.softmax(x, axis=axis)

def _gelu(x):
    return jax.nn.gelu(x, approximate=True)

def _silu(x):
    return jax.nn.silu(x)

def _sigmoid(x):
    return jax.nn.sigmoid(x)

def _layernorm(x, axis=-1, eps=1e-05):
    m = jnp.mean(x, axis=axis, keepdims=True)
    v = jnp.var(x, axis=axis, keepdims=True)
    return (x - m) / jnp.sqrt(v + eps)

def _scatter_add(tgt, idx, src, axis=0):
    return tgt.at[idx].add(src)

def _segment_sum(src, seg, n):
    return jax.ops.segment_sum(src, seg, n)
kernel_name = 'mk_flamingo_gated_d1_seqx_r4_9b02d5'

def setup_inputs(seed: int=0):
    np.random.seed(seed)
    _w = jnp.asarray

    def _rec_inputs():
        import jax
        import jax.numpy as jnp
        _rk = jax.random.key(seed)
        x = -0.000929 + 1 * jax.random.normal(jax.random.fold_in(_rk, 1), (1, 2048, 256), jnp.float32)
        _lenS = 2048 - jax.random.randint(jax.random.fold_in(_rk, 7), (1,), 0, max(1, 2048 // 4) + 1, jnp.int32)
        _lenS2 = 1601 - jax.random.randint(jax.random.fold_in(_rk, 8), (1,), 0, max(1, 1601 // 4) + 1, jnp.int32)
        _ctx_1024P = jax.random.normal(jax.random.fold_in(_rk, 11), (1, 16, 256), jnp.float32)
        _ctx_1024c = jax.random.dirichlet(jax.random.fold_in(_rk, 511), 0.3 * jnp.ones((16,), jnp.float32), (1, 1601))
        _ctx_1024t = jnp.einsum('bsk,bkd->bsd', _ctx_1024c, _ctx_1024P)
        _ctx_1024t = _ctx_1024t * jax.lax.rsqrt(jnp.mean(jnp.square(_ctx_1024t)) + 1e-12) * 0.953939
        ctx_1024 = -1.52775e-05 + 0.999936 * (_ctx_1024t + 0.3 * jax.random.normal(jax.random.fold_in(_rk, 611), (1, 1601, 256), jnp.float32))
        _g = jax.random.normal(jax.random.fold_in(_rk, 9001), (2, 1), jnp.float32)
        _g = jnp.sign(_g) * jnp.maximum(jnp.abs(_g), 1.0) + (_g == 0) * 1.0
        g_xattn = _g[0]
        g_ffn = _g[1]
        return (x, ctx_1024, g_xattn, g_ffn)
    x, ctx_1024, g_xattn, g_ffn = _rec_inputs()

    def _L0_xattn_setup():
        import jax, jax.numpy as jnp
        import numpy as np
        DIM = 256
        H = 16
        D = 64
        INNER = H * D
        EPS = 1e-05

        def layernorm(x, w, b):
            mu = jnp.mean(x, axis=-1, keepdims=True)
            var = jnp.var(x, axis=-1, keepdims=True)
            return (x - mu) * jax.lax.rsqrt(var + EPS) * w + b
        key = jax.random.key(seed)
        ks = jax.random.split(key, 8)
        B, N, S = (4, 64, 2048)
        s = 1.0 / np.sqrt(DIM)
        return {'latents': jax.random.normal(ks[0], (B, N, DIM), jnp.float32), 'context': jax.random.normal(ks[1], (B, S, DIM), jnp.float32), 'ln_l_w': jnp.ones((DIM,), jnp.float32), 'ln_l_b': jnp.zeros((DIM,), jnp.float32), 'ln_c_w': jnp.ones((DIM,), jnp.float32), 'ln_c_b': jnp.zeros((DIM,), jnp.float32), 'Wq': jax.random.normal(ks[2], (DIM, INNER), jnp.float32) * s, 'Wkv': jax.random.normal(ks[3], (DIM, 2 * INNER), jnp.float32) * s, 'Wo': jax.random.normal(ks[4], (INNER, DIM), jnp.float32) * (1.0 / np.sqrt(INNER)), 'bo': jnp.zeros((DIM,), jnp.float32)}
    _L0_xattn_all = _L0_xattn_setup()
    _L0_xattn_in = {k: v for k, v in _L0_xattn_all.items() if k in ('ln_l_w', 'ln_l_b', 'ln_c_w', 'ln_c_b', 'Wq', 'Wkv', 'Wo', 'bo')}
    del _L0_xattn_all

    def _L0_ffn_setup():
        import jax, jax.numpy as jnp
        import numpy as np
        BLOCK = 32
        W_BITS = 4
        ACT_BITS = 16

        def act_qdq(x):
            qmax = 2.0 ** (ACT_BITS - 1) - 1.0
            scale = jnp.maximum(jnp.max(jnp.abs(x)) / qmax, 1e-12)
            return jnp.clip(jnp.round(x / scale), -qmax - 1.0, qmax) * scale

        def fixed_qdq_u16(x):
            scale = 1.0 / 65536.0
            return jnp.clip(jnp.round(x / scale), 0.0, 65535.0) * scale

        def lpbq_dequant(w):
            O, I = w.shape
            qmax = 2.0 ** (W_BITS - 1) - 1.0
            wb = w.reshape(O, I // BLOCK, BLOCK)
            s = jnp.maximum(jnp.max(jnp.abs(wb), axis=-1, keepdims=True) / qmax, 1e-12)
            wq = jnp.clip(jnp.round(wb / s), -qmax - 1.0, qmax) * s
            return wq.reshape(O, I)
        key = jax.random.key(seed)
        k1, k2, k3, k4 = jax.random.split(key, 4)
        B, S, H, I = (2, 1024, 256, 768)
        x = jax.random.normal(k1, (B, S, H), jnp.float32)
        w_gate = jax.random.normal(k2, (I, H), jnp.float32) * 0.02
        w_up = jax.random.normal(k3, (I, H), jnp.float32) * 0.02
        w_down = jax.random.normal(k4, (H, I), jnp.float32) * 0.02
        return {'x': x, 'w_gate': w_gate, 'w_up': w_up, 'w_down': w_down}
    _L0_ffn_all = _L0_ffn_setup()
    _L0_ffn_in = {k: v for k, v in _L0_ffn_all.items() if k in ('w_gate', 'w_up', 'w_down')}
    del _L0_ffn_all
    return {'x': x, 'ctx_1024': ctx_1024, 'g_xattn': g_xattn, 'g_ffn': g_ffn, 'L0_xattn_ln_l_w': _L0_xattn_in['ln_l_w'], 'L0_xattn_ln_l_b': _L0_xattn_in['ln_l_b'], 'L0_xattn_ln_c_w': _L0_xattn_in['ln_c_w'], 'L0_xattn_ln_c_b': _L0_xattn_in['ln_c_b'], 'L0_xattn_Wq': _L0_xattn_in['Wq'], 'L0_xattn_Wkv': _L0_xattn_in['Wkv'], 'L0_xattn_Wo': _L0_xattn_in['Wo'], 'L0_xattn_bo': _L0_xattn_in['bo'], 'L0_ffn_w_gate': _L0_ffn_in['w_gate'], 'L0_ffn_w_up': _L0_ffn_in['w_up'], 'L0_ffn_w_down': _L0_ffn_in['w_down']}

def reference(x, ctx_1024, g_xattn, g_ffn, L0_xattn_ln_l_w, L0_xattn_ln_l_b, L0_xattn_ln_c_w, L0_xattn_ln_c_b, L0_xattn_Wq, L0_xattn_Wkv, L0_xattn_Wo, L0_xattn_bo, L0_ffn_w_gate, L0_ffn_w_up, L0_ffn_w_down):
    import jax
    import jax.numpy as jnp

    def _L0_xattn_ref(latents, context, ln_l_w, ln_l_b, ln_c_w, ln_c_b, Wq, Wkv, Wo, bo):
        import jax, jax.numpy as jnp
        import numpy as np
        DIM = 256
        H = 16
        D = 64
        INNER = H * D
        EPS = 1e-05

        def layernorm(x, w, b):
            mu = jnp.mean(x, axis=-1, keepdims=True)
            var = jnp.var(x, axis=-1, keepdims=True)
            return (x - mu) * jax.lax.rsqrt(var + EPS) * w + b
        b, n, _ = latents.shape
        s = context.shape[1]
        lat = layernorm(latents, ln_l_w, ln_l_b)
        ctx = layernorm(context, ln_c_w, ln_c_b)
        q = (lat @ Wq).reshape(b, n, H, D).transpose(0, 2, 1, 3)
        kv = ctx @ Wkv
        k, v = jnp.split(kv, 2, axis=-1)
        k = k.reshape(b, s, H, D).transpose(0, 2, 1, 3)
        v = v.reshape(b, s, H, D).transpose(0, 2, 1, 3)
        scale = D ** (-0.5)
        attn = jnp.einsum('bhnd,bhsd->bhns', q, k) * scale
        attn = jnp.clip(attn, -11.0, 11.0)
        attn = jax.nn.softmax(attn, axis=-1)
        out = jnp.einsum('bhns,bhsd->bhnd', attn, v)
        out = out.transpose(0, 2, 1, 3).reshape(b, n, INNER)
        return out @ Wo + bo

    def _L0_ffn_ref(x, w_gate, w_up, w_down):
        import jax, jax.numpy as jnp
        import numpy as np
        BLOCK = 32
        W_BITS = 4
        ACT_BITS = 16

        def act_qdq(x):
            qmax = 2.0 ** (ACT_BITS - 1) - 1.0
            scale = jnp.maximum(jnp.max(jnp.abs(x)) / qmax, 1e-12)
            return jnp.clip(jnp.round(x / scale), -qmax - 1.0, qmax) * scale

        def fixed_qdq_u16(x):
            scale = 1.0 / 65536.0
            return jnp.clip(jnp.round(x / scale), 0.0, 65535.0) * scale

        def lpbq_dequant(w):
            O, I = w.shape
            qmax = 2.0 ** (W_BITS - 1) - 1.0
            wb = w.reshape(O, I // BLOCK, BLOCK)
            s = jnp.maximum(jnp.max(jnp.abs(wb), axis=-1, keepdims=True) / qmax, 1e-12)
            wq = jnp.clip(jnp.round(wb / s), -qmax - 1.0, qmax) * s
            return wq.reshape(O, I)
        x = act_qdq(x)
        up = act_qdq(x @ lpbq_dequant(w_up).T)
        gate = act_qdq(x @ lpbq_dequant(w_gate).T)
        sig = fixed_qdq_u16(jax.nn.sigmoid(gate))
        gate = act_qdq(gate * sig)
        o = act_qdq(gate * up)
        return o @ lpbq_dequant(w_down).T
    x = x + jnp.tanh(g_xattn[0]) * _L0_xattn_ref(_layernorm(x, axis=-1), ctx_1024, L0_xattn_ln_l_w, L0_xattn_ln_l_b, L0_xattn_ln_c_w, L0_xattn_ln_c_b, L0_xattn_Wq, L0_xattn_Wkv, L0_xattn_Wo, L0_xattn_bo)
    x = x + jnp.tanh(g_ffn[0]) * _L0_ffn_ref(_layernorm(x, axis=-1), L0_ffn_w_gate, L0_ffn_w_up, L0_ffn_w_down)
    return x

_drawn_inputs = setup_inputs


def setup_inputs(seed=0):
    import zlib

    import numpy as np

    out = dict(_drawn_inputs(seed))
    spreads = {'L0_xattn_ln_l_w': (1.0, 0.59),
     'L0_xattn_ln_l_b': (0.0, 0.628),
     'L0_xattn_ln_c_w': (1.0, 0.2),
     'L0_xattn_ln_c_b': (0.0, 0.1),
     'L0_xattn_bo': (0.0, 0.1)}
    factors = {}
    for name, (base, spread) in spreads.items():
        noise = np.random.default_rng([zlib.crc32(name.encode()), seed]).standard_normal(out[name].shape)
        drawn = base * np.exp(spread * noise) if base else spread * noise
        out[name] = jnp.asarray(drawn.astype(out[name].dtype))
    for name, factor in factors.items():
        out[name] = (out[name] * factor).astype(out[name].dtype)
    return out
```

```python
from contextlib import ExitStack

import concourse.bass as bass
from concourse import mybir

ALU = mybir.AluOpType
ACT = mybir.ActivationFunctionType
AX_X = mybir.AxisListType.X
F32 = mybir.dt.float32
F32R = mybir.dt.float32r

P = 128
N, S, DM = 2048, 1601, 256
H, DH = 16, 64
FF = 768
QB = 32
KT = DM // P
PAIRS = H // 2
NB = 512
NBS = N // NB
NT = N // P
ST = -(-S // P)
SLAST = S - (ST - 1) * P
SPAD = S + 1
SB = -(-S // NB)
SEGS = PAIRS * NBS
LOOP0, LOOPS, UNROLL = 1, 3, 8
TAIL0 = LOOP0 + LOOPS * UNROLL
E_BUFS = 4
EPS = 1e-5
CLIP = 11.0
EXP_LO, EXP_HI = 1.6701700790245659e-05, 59874.14171519782
MAGIC = 12582912.0
QMAX = 32767.0
WMAX = 7.0
U16 = 65536.0
FT = FF // P
WBLK = 18 * DM // QB


def rows_of(st):
    return P if st < ST - 1 else SLAST


def cols_of(b):
    return min(NB, S - b * NB)


class Seg:

    def __init__(self, t0, i=None):
        self.t0, self.i = t0, i

    def count(self, per_segment, c):
        v = per_segment * self.t0 + c
        return v if self.i is None else v + per_segment * UNROLL * self.i

    def next(self):
        return Seg(self.t0 + 1, self.i)


def segment_jobs(t):
    jobs = []
    if t >= 1:
        jobs.append((1, ("den", t - 1)))
    if t + 1 < SEGS:
        jobs.append((3, ("q", t + 1)))
    p = t // NBS + 1
    if p < PAIRS:
        jobs.append((6, ("k", p, t % NBS)))
    if t >= 1:
        jobs += [(8, ("y", t - 1, 0)), (10, ("y", t - 1, 1))]
    if p < PAIRS:
        jobs.append((11, ("v", p, t % NBS)))
    return jobs


def job_table():
    order = [("cT", b, k) for b in range(SB) for k in range(KT)]
    order += [("lT", 0, k) for k in range(KT)] + [("q", 0)]
    order += [("k", 0, b) for b in range(SB)] + [("v", 0, b) for b in range(SB)]
    order += [("lT", b, k) for b in range(1, NBS) for k in range(KT)]
    order += [("wT", j) for j in range(9)]
    for t in range(SEGS):
        order += [key for _, key in segment_jobs(t)]
    order += [("den", SEGS - 1), ("y", SEGS - 1, 0), ("y", SEGS - 1, 1)]
    return {key: n for n, key in enumerate(order)}


JOBS = job_table()
PER_LOOP = 6 * UNROLL // 2


def bank_of(key):
    return JOBS[key] % 2


def place_of(key, seg):
    n = JOBS[key] // 2
    return n if seg is None or seg.i is None else n + PER_LOOP * seg.i


def attention_ffn(nc, x, ctx_rows, g_xattn, g_ffn, ln_l_w, ln_l_b, ln_c_w, ln_c_b,
                  Wq, Wkv, Wo, bo, w_gate, w_up, w_down, out):
    with ExitStack() as ctx:
        def sb(name, shape, dt=F32, stack=ctx):
            return stack.enter_context(nc.sbuf_tensor(name, shape, dt))

        def sem(name):
            return ctx.enter_context(nc.semaphore(name))

        xacc = sb("xacc", [P, NT, DM])
        z = sb("z", [P, NT, DM])
        ident = sb("ident", [P, P])
        ones = sb("ones", [P, P])
        gates = sb("gates", [P, 2])
        tg = sb("tg", [P, 2])
        cols = sb("cols", [P, 4, KT])
        bo_t = sb("bo_t", [P, DM])
        stats = sb("stats", [P, NT, 6])
        mv = sb("mv", [P, 3, NT, 2])
        lnt = sb("lnt", [P, 3, 4, NT])
        wgu = sb("wgu", [P, 2, KT, FF])
        wdT = sb("wdT", [P, FT, DM])

        with ExitStack() as att:
            latT = sb("latT", [P, KT, N], stack=att)
            ctxT = sb("ctxT", [P, KT, S], stack=att)
            vb = sb("vb", [P, 2, ST, P], stack=att)
            qb = sb("qb", [P, 2, 2, NB], F32R, stack=att)
            e_buf = sb("e_buf", [P, E_BUFS, 2, NB], stack=att)
            acc = sb("acc", [P, 2, 2, NB], stack=att)
            rden = sb("rden", [P, NB], stack=att)
            oT = sb("oT", [P, 2, NB], stack=att)
            wst = sb("wst", [P, 2, 3, KT, P], stack=att)
            wo_raw = sb("wo_raw", [P, 2, DM], stack=att)
            wo_g = sb("wo_g", [P, 2, DM], stack=att)
            kb_even = sb("kb_even", [P, 2, 2, SPAD], F32R, stack=att)
            with ExitStack() as tmp:
                wraw = sb("wraw", [P, 18, DM], stack=tmp)
                wsc = sb("wsc", [P, 3, WBLK], stack=tmp)
            kb = (kb_even, sb("kb_odd", [P, 2, 2, SPAD], F32R, stack=att))
            e_flat = e_buf[:, :, :, :].rearrange("p a b n -> p (a b n)")
            crow = e_flat[:, 0:ST * DM].rearrange("p (t d) -> p t d", d=DM)

        with ExitStack() as ffn:
            hT = sb("hT", [P, KT, N], stack=ffn)
            up = sb("up", [P, FT, N], stack=ffn)
            gt = sb("gt", [P, FT, N], stack=ffn)
            sg = sb("sg", [P, 2, N], stack=ffn)
            fst = sb("fst", [P, 5, 32], stack=ffn)
            fsc = sb("fsc", [P, 5, 4], stack=ffn)
            frow = sb("frow", [1, 2, P], stack=ffn)

        psum = nc.psum_tensor("ps", [P, 8, NB], F32)
        ps = ctx.enter_context(psum)
        ps_s, ps_o, ps_m = ps[:, 0:4, :], ps[:, 4:6, :], ps[:, 6:8, :]
        sc = ps_s.rearrange("p (a h) n -> p a h n", h=2)

        in_ctx, in_x = sem("in_ctx"), [sem(f"in_x{b}") for b in range(NBS)]
        in_small, in_w = sem("in_small"), sem("in_w")
        w_loaded = [sem("w_loaded0"), sem("w_loaded1")]
        ident_zero, ident_done, const_done = sem("ident_zero"), sem("ident_done"), sem("const_done")
        dve_chain, act_chain = sem("dve_chain"), sem("act_chain")
        var_ready, root_ready = sem("var_ready"), sem("root_ready")
        ctx_norm, lat_norm, wq_done = sem("ctx_norm"), sem("lat_norm"), sem("wq_done")
        tanh_done, wo_scaled, bias_added, bias_scaled = sem("tanh_done"), sem("wo_scaled"), sem("bias_added"), sem("bias_scaled")
        job_ready = [sem("job_ready0"), sem("job_ready1")]
        job_taken = [sem("job_taken0"), sem("job_taken1")]
        q_high, k_high = sem("q_high"), sem("k_high")
        scores_ready, exp_done, clip_done, pv_done = sem("scores_ready"), sem("exp_done"), sem("clip_done"), sem("pv_done")
        sum_a, sum_b = sem("sum_a"), sem("sum_b")
        norm_done = sem("norm_done")
        h_norm, hT_ready, hT_done = sem("h_norm"), sem("hT_ready"), sem("hT_done")
        col_ready, colT_ready, max_ready, bc_ready = sem("col_ready"), sem("colT_ready"), sem("max_ready"), sem("bc_ready")
        scale_done = sem("scale_done")
        f1_ready, f1_out = sem("f1_ready"), sem("f1_out")
        gq_done, sig_done, oq_done = sem("gq_done"), sem("sig_done"), sem("oq_done")
        f2_ready, f2_out, stored = sem("f2_ready"), sem("f2_out"), sem("stored")

        block = ctx.enter_context(nc.Block())

        def await_job(eng, key, seg=None):
            eng.wait_ge(job_ready[bank_of(key)], place_of(key, seg) + 1)

        def await_taken(eng, key, seg=None):
            eng.wait_ge(job_taken[bank_of(key)], place_of(key, seg) + 1)

        def await_all_taken(eng, keys, seg=None):
            for bank in range(2):
                mine = [key for key in keys if bank_of(key) == bank]
                if mine:
                    await_taken(eng, max(mine, key=JOBS.get), seg)

        def segments(eng, run):
            run(Seg(0))
            with eng.Fori(0, LOOPS) as i:
                for t0 in range(LOOP0, LOOP0 + UNROLL):
                    run(Seg(t0, i))
            for t in range(TAIL0, SEGS):
                run(Seg(t))

        @block.sync
        def _(sp):
            full = (ST - 1) * P
            sp.dma_start(crow[:, 0:ST - 1, :], ctx_rows[0, 0:full, :].rearrange("(t p) d -> p t d", p=P)).then_inc(in_ctx, 16)
            sp.dma_start(crow[0:SLAST, ST - 1, :], ctx_rows[0, full:S, :]).then_inc(in_ctx, 16)
            for b in range(NBS):
                sp.dma_start(xacc[:, 4 * b:4 * b + 4, :],
                             x[0, b * NB:(b + 1) * NB, :].rearrange("(t p) d -> p t d", p=P)).then_inc(in_x[b], 16)
            for n, a in enumerate((ln_l_w, ln_l_b, ln_c_w, ln_c_b)):
                sp.dma_start(cols[:, n, :], a.rearrange("(k p) -> p k", k=KT), allow_slow_non_contiguous=True).then_inc(in_small, 16)
            for n, a in enumerate((g_xattn, g_ffn)):
                sp.dma_start(gates[:, n:n + 1], a.rearrange("(a n) -> a n", a=1).to_broadcast([P, 1])).then_inc(in_small, 16)
            sp.dma_start(bo_t[:, :], bo.rearrange("(a n) -> a n", a=1).to_broadcast([P, DM])).then_inc(in_small, 16)

            def load_pair(p, parity):
                for n, (w, at) in enumerate(((Wq, 0), (Wkv, 0), (Wkv, H * DH))):
                    sp.dma_start(wst[:, parity, n, :, :],
                                 w[:, bass.ds(P * p + at, P)].rearrange("(k q) n -> q k n", q=P)).then_inc(w_loaded[parity], 16)
                sp.dma_start(wo_raw[:, parity, :], Wo[bass.ds(P * p, P), :]).then_inc(w_loaded[parity], 16)

            load_pair(0, 0)
            load_pair(1, 1)
            for n, w in enumerate((w_up, w_gate)):
                sp.dma_start(wraw[:, 6 * n:6 * n + 6, :], w.rearrange("(t p) d -> p t d", p=P)).then_inc(in_w, 16)
            sp.dma_start(wraw[:, 12:18, :].rearrange("p (t j) d -> p t (j d)", t=2),
                         w_down.rearrange("(t p) f -> p t f", p=P)).then_inc(in_w, 16)

            def run(seg):
                if seg.t0 % NBS != NBS - 1 or (seg.t0 + 5) // NBS >= PAIRS:
                    return
                p = (seg.t0 + 5) // NBS
                await_taken(sp, ("q", seg.t0), seg)
                sp.wait_ge(wo_scaled, p - 1 if seg.i is None else p - 1 + 2 * seg.i)
                load_pair(p if seg.i is None else p + 2 * seg.i, p % 2)

            segments(sp, run)
            for g in range(NT // 2):
                sp.wait_ge(f2_out, g + 1)
                sp.dma_start(out[0, 2 * g * P:(2 * g + 2) * P, :].rearrange("(t p) d -> p t d", p=P),
                             z[:, 2 * g:2 * g + 2, :]).then_inc(stored, 16)
            sp.wait_ge(stored, 16 * (NT // 2))

        @block.gpsimd
        def _(pool):
            pool.memset(ident[:, :], 0.0).then_inc(ident_zero, 1)
            pool.wait_ge(ident_zero, 1)
            pool.affine_select(out=ident[:, :], in_=ident[:, :], compare_op=ALU.not_equal, fill=1.0, base=0,
                               pattern=[[-1, P]], channel_multiplier=1).then_inc(ident_done, 1)
            pool.wait_ge(tanh_done, 1)
            pool.wait_ge(in_small, 16 * 7)
            pool.tensor_scalar(bo_t[:, :], bo_t[:, :], tg[:, 0:1], None, ALU.mult).then_inc(bias_scaled, 1)
            pool.wait_ge(bias_scaled, 1)

            def run(seg):
                t0 = seg.t0
                if t0 % NBS == 0:
                    p = t0 // NBS
                    pool.wait_ge(w_loaded[p % 2], (p // 2 + 1) * 64 if seg.i is None else (p // 2 + 1) * 64 + 64 * seg.i)
                    if t0 > NBS:
                        await_job(pool, ("y", t0 - NBS - 1, 1), seg)
                    pool.tensor_tensor(wo_g[:, p % 2, :], wo_raw[:, p % 2, :], tg[:, 0:1].to_broadcast([P, DM]),
                                       ALU.mult).then_inc(wo_scaled, 1)
                for st in range(1, ST):
                    r = rows_of(st)
                    pool.wait_ge(clip_done, seg.count(ST, st + 1))
                    if st == 1:
                        if t0 >= 2:
                            await_job(pool, ("den", t0 - 2), seg)
                        a = e_buf[:, (ST * t0) % E_BUFS, 1, :]
                    else:
                        pool.wait_ge(sum_b, seg.count(ST - 1, st - 1))
                        a = acc[0:r, t0 % 2, 1, :]
                    pool.tensor_tensor(acc[0:r, t0 % 2, 1, :], a, e_buf[0:r, (ST * t0 + st) % E_BUFS, 1, :],
                                       ALU.add).then_inc(sum_b, 1)
                    if t0 == 0 and st % 3 == 0:
                        b = st // 3 - 1
                        pool.wait_ge(lat_norm, NT)
                        for i in range(4):
                            pool.tensor_tensor(xacc[:, 4 * b + i, :], xacc[:, 4 * b + i, :], bo_t[:, :], ALU.add).then_inc(bias_added, 1)

            segments(pool, run)

        @block.scalar
        def _(act):
            act.wait_ge(in_small, 16 * 7)
            nc.scalar.activation(tg[:, :], gates[:, :], ACT.Tanh).then_inc(tanh_done, 1)

            def root(n, w):
                act.wait_ge(var_ready, n + 1)
                nc.scalar.activation(lnt[:, n, 1, 0:w], lnt[:, n, 0, 0:w], ACT.Sqrt).then_inc(root_ready, 1)

            def take_T(key, dst, n, w):
                k = key[2]
                await_job(act, key)
                nc.scalar.activation(dst[:, k, key[1] * NB:key[1] * NB + w], ps_m[:, bank_of(key), 0:w], ACT.Identity,
                                     bias=cols[:, n + 1, k:k + 1], scale=cols[:, n, k:k + 1]).then_inc(job_taken[bank_of(key)], 1)

            def q_take(seg, t):
                await_job(act, ("q", t), seg)
                for h in range(2):
                    nc.scalar.copy(qb[0:DH, t % 2, h, :], ps_m[DH * h:DH * h + DH, bank_of(("q", t)), :]).then_inc(q_high, 1)

            def k_take(seg, p, b):
                w = cols_of(b)
                await_job(act, ("k", p, b), seg)
                for h in range(2):
                    for half in range(2):
                        nc.scalar.copy(kb[p % 2][DH * half:DH * half + DH, h, 0, b * NB:b * NB + w],
                                       ps_m[DH * h:DH * h + DH, bank_of(("k", p, b)), 0:w]).then_inc(k_high, 1)

            def v_take(seg, p, b):
                key = ("v", p, b)
                await_job(act, key, seg)
                if b < SB - 1:
                    nc.scalar.copy(vb[:, p % 2, 4 * b:4 * b + 4, :],
                                   ps_m[:, bank_of(key), :].rearrange("p (t n) -> p t n", n=P)).then_inc(job_taken[bank_of(key)], 1)
                else:
                    nc.scalar.copy(vb[0:SLAST, p % 2, ST - 1, :], ps_m[0:SLAST, bank_of(key), 0:P]).then_inc(job_taken[bank_of(key)], 1)

            root(0, ST)
            for b in range(SB):
                for k in range(KT):
                    take_T(("cT", b, k), ctxT, 2, cols_of(b))
            root(1, NT)
            for k in range(KT):
                take_T(("lT", 0, k), latT, 0, NB)
            q_take(None, 0)
            for b in range(SB):
                k_take(None, 0, b)
            for b in range(SB):
                v_take(None, 0, b)
            for b in range(1, NBS):
                for k in range(KT):
                    take_T(("lT", b, k), latT, 0, NB)
            for j in range(9):
                await_job(act, ("wT", j))
                bank = ps_m[:, bank_of(("wT", j)), :]
                if j < 6:
                    m, k, f = j // 3, 0, 0
                    dst = wgu[:, m, :, :].rearrange("p k f -> p (k f)")[:, (j % 3) * NB:(j % 3 + 1) * NB]
                else:
                    dst = wdT[:, :, :].rearrange("p f d -> p (f d)")[:, (j - 6) * NB:(j - 5) * NB]
                nc.scalar.copy(dst, bank).then_inc(job_taken[bank_of(("wT", j))], 1)

            def run(seg):
                t0 = seg.t0
                for st in range(ST):
                    r, g = rows_of(st), ST * t0 + st
                    act.wait_ge(scores_ready, seg.count(ST, st + 1))
                    if g >= E_BUFS:
                        act.wait_ge(pv_done, seg.count(ST, st + 1 - E_BUFS))
                        back = Seg(t0 if st >= E_BUFS else t0 - 1, seg.i)
                        s0 = max((st - E_BUFS) % ST, 1)
                        act.wait_ge(sum_a, back.count(ST - 1, s0))
                        act.wait_ge(sum_b, back.count(ST - 1, s0))
                    nc.scalar.activation(e_buf[0:r, g % E_BUFS, :, :], sc[0:r, g % 2, :, :], ACT.Exp,
                                         scale=float(DH) ** -0.5).then_inc(exp_done, 1)
                    p = t0 // NBS + 1
                    if st == 5 and t0 + 1 < SEGS:
                        q_take(seg, t0 + 1)
                    if st == 8 and p < PAIRS:
                        k_take(seg, p, t0 % NBS)
                    if st == 12 and p < PAIRS:
                        v_take(seg, p, t0 % NBS)

            segments(act, run)

            root(2, NT)
            for c in range(2 * FT * NBS):
                m, f, b = c // (FT * NBS), c // NBS % FT, c % NBS
                act.wait_ge(f1_ready, c + 1)
                if c == 0:
                    act.wait_ge(scale_done, 1)
                dst = (up, gt)[m]
                nc.scalar.activation(dst[:, f, b * NB:(b + 1) * NB], ps[:, c % 8, :], ACT.Copy,
                                     scale=fsc[:, 0, 1:2]).then_inc(f1_out, 1)
            for f in range(FT):
                act.wait_ge(gq_done, f + 1)
                if f >= 2:
                    act.wait_ge(oq_done, f - 1)
                nc.scalar.activation(sg[:, f % 2, :], gt[:, f, :], ACT.Sigmoid).then_inc(sig_done, 1)

        @block.vector
        def _(dve):
            chain = [0]

            def link(ins):
                chain[0] += 1
                ins.then_inc(dve_chain, 1)
                dve.wait_ge(dve_chain, chain[0])

            def inverse_root(n, w, c1, c0):
                a, s, r, u = (lnt[:, n, j, 0:w] for j in range(4))
                dve.tensor_scalar(a, mv[:, n, 0:w, 1], c1, c0, ALU.mult, ALU.add).then_inc(var_ready, 1)
                dve.wait_ge(root_ready, n + 1)
                link(dve.reciprocal(r, s))
                link(dve.tensor_tensor(u, r, r, ALU.mult))
                link(dve.tensor_tensor(u, u, a, ALU.mult))
                link(dve.tensor_scalar(u, u, -0.5, 1.5, ALU.mult, ALU.add))
                link(dve.tensor_tensor(r, r, u, ALU.mult))

            def moments(n, t, src):
                r = src.shape[0]
                link(dve.bn_stats(stats[0:r, t, :], src))
                return dve.bn_aggr(mv[0:r, n, t, :], stats[0:r, t, :])

            def normalise(dst, src, n, t):
                r = src.shape[0]
                return dve.tensor_scalar(dst, src, mv[0:r, n, t, 0:1], lnt[0:r, n, 2, t:t + 1], ALU.subtract, ALU.mult)

            dve.memset(ones[:, :], 1.0).then_inc(const_done, 1)
            link(dve.memset(mv[:, :, :, :], 1.0))
            dve.wait_ge(in_ctx, 32)
            for t in range(ST):
                ins = moments(0, t, crow[0:rows_of(t), t, :])
            link(ins)
            inverse_root(0, ST, 1.0, EPS)
            for t in range(ST):
                normalise(crow[0:rows_of(t), t, :], crow[0:rows_of(t), t, :], 0, t).then_inc(ctx_norm, 1)
            for t in range(NT):
                if t % 4 == 0:
                    dve.wait_ge(in_x[t // 4], 16)
                ins = moments(1, t, xacc[:, t, :])
            link(ins)
            inverse_root(1, NT, 1.0 + EPS, EPS * EPS)
            for t in range(NT):
                normalise(z[:, t, :], xacc[:, t, :], 1, t).then_inc(lat_norm, 1)

            def q_low(seg, t):
                bank = bank_of(("q", t))
                for h in range(2):
                    dve.wait_ge(q_high, 2 * (t if seg is None else seg.t0 + 1) + 1 + h + (0 if seg is None or seg.i is None else 2 * UNROLL * seg.i))
                    ins = dve.tensor_tensor(qb[DH:P, t % 2, h, :], ps_m[DH * h:DH * h + DH, bank, :],
                                            qb[0:DH, t % 2, h, :].bitcast(F32), ALU.subtract)
                ins.then_inc(job_taken[bank], 1)

            def k_low(seg, p, b, h):
                w, bank = cols_of(b), bank_of(("k", p, b))
                done = 4 * (b + (p * NBS if seg is None else seg.t0 - seg.t0 % NBS + NBS)) + 2 * h + 2
                dve.wait_ge(k_high, done + (0 if seg is None or seg.i is None else 4 * UNROLL * seg.i))
                for half in range(2):
                    lo, hi = DH * half, DH * half + DH
                    ins = dve.tensor_tensor(kb[p % 2][lo:hi, h, 1, b * NB:b * NB + w], ps_m[DH * h:DH * h + DH, bank, 0:w],
                                            kb[p % 2][lo:hi, h, 0, b * NB:b * NB + w].bitcast(F32), ALU.subtract)
                if h == 1:
                    ins.then_inc(job_taken[bank], 1)

            q_low(None, 0)
            for b in range(SB):
                for h in range(2):
                    k_low(None, 0, b, h)

            dve.wait_ge(in_w, 48)
            blocks = wraw[:, :, :].rearrange("p t (n e) -> p (t n) e", e=QB)
            link(dve.tensor_reduce(wsc[:, 0, :], blocks, AX_X, ALU.max, apply_absolute_value=True))
            link(dve.tensor_scalar(wsc[:, 1, :], wsc[:, 0, :], 1.0 / WMAX, 1e-12, ALU.mult, ALU.max))
            link(dve.reciprocal(wsc[:, 2, :], wsc[:, 1, :]))
            link(dve.tensor_tensor(blocks, blocks, wsc[:, 2, :].unsqueeze(2).to_broadcast([P, WBLK, QB]), ALU.mult))
            link(dve.tensor_scalar(wraw[:, :, :], wraw[:, :, :], MAGIC, MAGIC, ALU.add, ALU.subtract))
            dve.tensor_tensor(blocks, blocks, wsc[:, 1, :].unsqueeze(2).to_broadcast([P, WBLK, QB]), ALU.mult).then_inc(wq_done, 1)

            def add_a(seg, st):
                t0, r = seg.t0, rows_of(st)
                if st == 1:
                    a = e_buf[:, (ST * t0) % E_BUFS, 0, :]
                else:
                    a = acc[0:r, t0 % 2, 0, :]
                    dve.wait_ge(sum_a, seg.count(ST - 1, st - 1))
                dve.wait_ge(clip_done, seg.count(ST, st + 1))
                dve.tensor_tensor(acc[0:r, t0 % 2, 0, :], a, e_buf[0:r, (ST * t0 + st) % E_BUFS, 0, :],
                                  ALU.add).then_inc(sum_a, 1)

            def invert(seg, t, c):
                bank, w = bank_of(("den", t)), NB // 4
                await_job(dve, ("den", t), seg)
                ins = dve.reciprocal(rden[:, c * w:(c + 1) * w], ps_m[:, bank, c * w:(c + 1) * w])
                if c == 3:
                    ins.then_inc(job_taken[bank], 1)

            def scale_out(seg, t):
                await_taken(dve, ("den", t), seg)
                dve.wait_ge(pv_done, Seg(t, seg.i).count(ST, ST))
                dve.tensor_tensor(oT[:, t % 2, :], ps_o[:, t % 2, :], rden[:, :], ALU.mult).then_inc(norm_done, 1)

            def add_y(seg, t, half):
                key = ("y", t, half)
                n0 = 4 * (t % NBS) + 2 * half
                await_job(dve, key, seg)
                if seg.t0 <= 4:
                    dve.wait_ge(bias_added, NT)
                dst = xacc[:, n0:n0 + 2, :]
                dve.tensor_tensor(dst, ps_m[:, bank_of(key), :].rearrange("p (t d) -> p t d", d=DM), dst,
                                  ALU.add).then_inc(job_taken[bank_of(key)], 1)

            def run(seg):
                t0 = seg.t0
                p = t0 // NBS + 1
                for st in range(ST):
                    r, g = rows_of(st), ST * t0 + st
                    dve.wait_ge(exp_done, seg.count(ST, st + 1))
                    tile = e_buf[0:r, g % E_BUFS, :, :]
                    dve.tensor_scalar(tile, tile, EXP_LO, EXP_HI, ALU.max, ALU.min).then_inc(clip_done, 1)
                    if st >= 2:
                        add_a(seg, st - 1)
                    elif st == 0 and t0 >= 1:
                        add_a(Seg(t0 - 1, seg.i), ST - 1)
                    if t0 >= 1 and 3 <= st <= 6:
                        invert(seg, t0 - 1, st - 3)
                    if st == 7 and t0 >= 1:
                        scale_out(seg, t0 - 1)
                    if st == 8 and t0 + 1 < SEGS:
                        q_low(seg, t0 + 1)
                    if st in (9, 10) and p < PAIRS:
                        k_low(seg, p, t0 % NBS, st - 9)
                    if st == 10 and t0 >= 1:
                        add_y(seg, t0 - 1, 0)
                    if st == 12 and t0 >= 1:
                        add_y(seg, t0 - 1, 1)

            segments(dve, run)
            end = Seg(SEGS)
            add_a(Seg(SEGS - 1), ST - 1)
            for c in range(4):
                invert(end, SEGS - 1, c)
            scale_out(end, SEGS - 1)
            add_y(end, SEGS - 1, 0)
            add_y(end, SEGS - 1, 1)
            last = ("y", SEGS - 1, 1)
            await_taken(dve, last)
            await_taken(dve, ("y", SEGS - 1, 0))

            for t in range(NT):
                ins = moments(2, t, xacc[:, t, :])
            link(ins)
            inverse_root(2, NT, 1.0, EPS)
            for t in range(NT):
                normalise(z[:, t, :], xacc[:, t, :], 2, t).then_inc(h_norm, 1)
            dve.wait_ge(h_norm, NT)

            def top(dst, src):
                return dve.tensor_reduce(dst, src, AX_X, ALU.max, apply_absolute_value=True)

            def scale_of(n, pieces):
                top(fsc[:, n, 0:1], fst[:, n, 0:pieces]).then_inc(col_ready, 1)
                dve.wait_ge(colT_ready, n + 1)
                link(top(frow[:, 1, 0:1], ps[0:1, 7, 0:P]))
                link(dve.tensor_scalar(frow[:, 0, 0:1], frow[:, 1, 0:1], 1.0 / QMAX, 1e-12, ALU.mult, ALU.max))
                dve.tensor_copy(frow[:, 0, 1:2], frow[:, 0, 0:1]).then_inc(max_ready, 1)
                dve.wait_ge(bc_ready, n + 1)
                link(dve.tensor_copy(fsc[:, n, 1:2], ps[:, 7, 0:1]))
                dve.reciprocal(fsc[:, n, 2:3], fsc[:, n, 1:2]).then_inc(scale_done, 1)
                dve.wait_ge(scale_done, n + 1)

            for b in range(4):
                ins = top(fst[:, 0, b:b + 1], z[:, 4 * b:4 * b + 4, :].rearrange("p t d -> p (t d)"))
            link(ins)
            scale_of(0, 4)
            for j in range(KT * NBS):
                k, b = j % KT, j // KT
                dve.wait_ge(hT_ready, j + 1)
                piece = hT[:, k, b * NB:(b + 1) * NB]
                link(dve.tensor_scalar(piece, ps[:, j % 4, :], fsc[:, 0, 2:3], MAGIC, ALU.mult, ALU.add))
                dve.tensor_scalar(piece, piece, MAGIC, None, ALU.subtract).then_inc(hT_done, 1)
            half = FT * NBS
            for m in range(2):
                src = (up, gt)[m]
                for c in range(half):
                    f, b = c // NBS, c % NBS
                    dve.wait_ge(f1_out, half * m + c + 1)
                    ins = top(fst[:, 1 + m, c:c + 1], src[:, f, b * NB:(b + 1) * NB])
                link(ins)
                scale_of(1 + m, half)
                if m == 0:
                    for f in range(FT):
                        link(dve.tensor_scalar(up[:, f, :], up[:, f, :], fsc[:, 1, 2:3], MAGIC, ALU.mult, ALU.add))
                        link(dve.tensor_scalar(up[:, f, :], up[:, f, :], MAGIC, fsc[:, 1, 1:2], ALU.subtract, ALU.mult))

            def quantise_gate(f):
                link(dve.tensor_scalar(gt[:, f, :], gt[:, f, :], fsc[:, 2, 2:3], MAGIC, ALU.mult, ALU.add))
                dve.tensor_scalar(gt[:, f, :], gt[:, f, :], MAGIC, fsc[:, 2, 1:2], ALU.subtract, ALU.mult).then_inc(gq_done, 1)

            quantise_gate(0)
            for f in range(FT):
                if f + 1 < FT:
                    quantise_gate(f + 1)
                dve.wait_ge(gq_done, f + 1)
                dve.wait_ge(sig_done, f + 1)
                s = sg[:, f % 2, :]
                link(dve.tensor_scalar(s, s, U16, MAGIC, ALU.mult, ALU.add))
                link(dve.tensor_scalar(s, s, MAGIC, U16 - 1.0, ALU.subtract, ALU.min))
                ins = dve.scalar_tensor_tensor(out=gt[:, f, :], in0=s, scalar=1.0 / U16, in1=gt[:, f, :],
                                               op0=ALU.mult, op1=ALU.mult)
                ins.then_inc(oq_done, 1)
                dve.wait_ge(oq_done, f + 1)
                ins = top(fst[:, 3, f:f + 1], gt[:, f, :])
            link(ins)
            scale_of(3, FT)
            for f in range(FT):
                link(dve.tensor_scalar(gt[:, f, :], gt[:, f, :], fsc[:, 3, 2:3], MAGIC, ALU.mult, ALU.add))
                link(dve.tensor_scalar(gt[:, f, :], gt[:, f, :], MAGIC, fsc[:, 3, 1:2], ALU.subtract, ALU.mult))
                link(dve.tensor_tensor(up[:, f, :], up[:, f, :], gt[:, f, :], ALU.mult))
                ins = top(fst[:, 4, f:f + 1], up[:, f, :])
            link(ins)
            scale_of(4, FT)
            link(dve.tensor_tensor(fsc[:, 4, 3:4], fsc[:, 4, 1:2], tg[:, 1:2], ALU.mult))
            for b in range(NBS):
                cols_b = slice(b * NB, (b + 1) * NB)
                link(dve.tensor_scalar(up[:, :, cols_b], up[:, :, cols_b], fsc[:, 4, 2:3], MAGIC, ALU.mult, ALU.add))
                dve.tensor_scalar(up[:, :, cols_b], up[:, :, cols_b], MAGIC, None, ALU.subtract).then_inc(oq_done, 1)
            for g in range(NT // 2):
                dve.wait_ge(f2_ready, g + 1)
                dve.scalar_tensor_tensor(out=z[:, 2 * g:2 * g + 2, :],
                                         in0=ps[:, g % 4, :].rearrange("p (t d) -> p t d", d=DM), scalar=fsc[:, 4, 3:4],
                                         in1=xacc[:, 2 * g:2 * g + 2, :], op0=ALU.mult, op1=ALU.add).then_inc(f2_out, 1)

        @block.tensor
        def _(pe):
            def bank_free(key, seg=None):
                n = place_of(key, seg)
                if JOBS[key] >= 2:
                    pe.wait_ge(job_taken[bank_of(key)], n)
                return ps_m[:, bank_of(key), :]

            def transposes(key, tiles):
                bank = bank_free(key)
                for i, (r, src) in enumerate(tiles):
                    ins = pe.transpose(bank[:, P * i:P * i + r], src, ident[0:r, 0:r])
                ins.then_inc(job_ready[bank_of(key)], 1)

            def q_job(seg, t, at):
                bank = bank_free(("q", t), seg)
                pe.wait_ge(w_loaded[at[0]], at[1])
                b = t % NBS
                for k in range(KT):
                    ins = pe.matmul(bank, wst[:, at[0], 0, k, :], latT[:, k, b * NB:(b + 1) * NB], start=(k == 0), stop=(k == KT - 1))
                ins.then_inc(job_ready[bank_of(("q", t))], 1)

            def k_job(seg, p, b, at):
                key, w = ("k", p, b), cols_of(b)
                bank = bank_free(key, seg)
                pe.wait_ge(w_loaded[at[0]], at[1])
                for k in range(KT):
                    ins = pe.matmul(bank[:, 0:w], wst[:, at[0], 1, k, :], ctxT[:, k, b * NB:b * NB + w], start=(k == 0), stop=(k == KT - 1))
                ins.then_inc(job_ready[bank_of(key)], 1)

            def v_job(seg, p, b, at):
                key = ("v", p, b)
                bank = bank_free(key, seg)
                for i, st in enumerate(range(4 * b, min(4 * b + 4, ST))):
                    r = rows_of(st)
                    for k in range(KT):
                        ins = pe.matmul(bank[0:r, P * i:P * i + P], ctxT[:, k, P * st:P * st + r], wst[:, at[0], 2, k, :],
                                        start=(k == 0), stop=(k == KT - 1))
                ins.then_inc(job_ready[bank_of(key)], 1)

            def den_job(seg, t):
                bank = bank_free(("den", t), seg)
                s = Seg(t, seg.i)
                pe.wait_ge(sum_a, s.count(ST - 1, ST - 1))
                pe.wait_ge(sum_b, s.count(ST - 1, ST - 1))
                for h in range(2):
                    ins = pe.matmul(bank[DH * h:DH * h + DH, :], ones[:, 0:DH], acc[:, t % 2, h, :], start=True, stop=True)
                ins.then_inc(job_ready[bank_of(("den", t))], 1)

            def y_job(seg, t, half):
                key = ("y", t, half)
                bank = bank_free(key, seg)
                s = Seg(t, seg.i)
                pe.wait_ge(norm_done, s.count(1, 1))
                p = t // NBS
                pe.wait_ge(wo_scaled, p + 1 if seg.i is None else p + 1 + 2 * seg.i)
                for m in range(2):
                    n0 = P * (2 * half + m)
                    ins = pe.matmul(bank[:, DM * m:DM * m + DM], oT[:, t % 2, n0:n0 + P], wo_g[:, p % 2, :], start=True, stop=True)
                ins.then_inc(job_ready[bank_of(key)], 1)

            def loaded(p, seg):
                v = 64 * (p // 2 + 1)
                return p % 2, v if seg is None or seg.i is None else v + 64 * seg.i

            def scores(seg, st):
                t0, r = seg.t0, rows_of(st)
                g, p = ST * t0 + st, t0 // NBS
                if st == 0:
                    keys = [("k", p, b) for b in range(SB)] if t0 % NBS == 0 else []
                    await_all_taken(pe, keys + [("q", t0)], seg)
                if g >= 2:
                    pe.wait_ge(exp_done, seg.count(ST, st - 1))
                for h in range(2):
                    for part in range(2):
                        ins = pe.matmul(sc[0:r, g % 2, h, :], kb[p % 2][:, h, part, P * st:P * st + r], qb[:, t0 % 2, h, :],
                                        start=(part == 0), stop=(part == 1))
                ins.then_inc(scores_ready, 1)

            def values(seg, st):
                t0, r = seg.t0, rows_of(st)
                g, p = ST * t0 + st, t0 // NBS
                if st % 4 == 0 and t0 % NBS == 0:
                    await_taken(pe, ("v", p, st // 4), seg)
                if st == 0 and t0 >= 2:
                    pe.wait_ge(norm_done, seg.count(1, -1))
                pe.wait_ge(clip_done, seg.count(ST, st + 1))
                for h in range(2):
                    ins = pe.matmul(ps_o[DH * h:DH * h + DH, t0 % 2, :], vb[0:r, p % 2, st, DH * h:DH * h + DH],
                                    e_buf[0:r, g % E_BUFS, h, :], start=(st == 0), stop=(st == ST - 1))
                ins.then_inc(pv_done, 1)

            pe.wait_ge(ident_done, 1)
            pe.wait_ge(const_done, 1)
            for b in range(SB):
                tiles = range(4 * b, min(4 * b + 4, ST))
                pe.wait_ge(ctx_norm, tiles[-1] + 1)
                for k in range(KT):
                    transposes(("cT", b, k), [(rows_of(t), crow[0:rows_of(t), t, P * k:P * k + P]) for t in tiles])

            def lat_transposes(b):
                pe.wait_ge(lat_norm, 4 * b + 4)
                for k in range(KT):
                    transposes(("lT", b, k), [(P, z[:, 4 * b + i, P * k:P * k + P]) for i in range(4)])

            lat_transposes(0)
            for k in range(KT):
                await_taken(pe, ("lT", 0, k))
                await_taken(pe, ("cT", SB - 1, k))
            q_job(None, 0, loaded(0, None))
            for b in range(SB):
                k_job(None, 0, b, loaded(0, None))
            for b in range(SB):
                v_job(None, 0, b, loaded(0, None))
            for b in range(1, NBS):
                lat_transposes(b)
            pe.wait_ge(wq_done, 1)
            for j in range(9):
                tiles = []
                for i in range(4):
                    n = 4 * (j if j < 6 else j - 6) + i
                    if j < 6:
                        m, k, f = n // 12, n // 6 % 2, n % 6
                        tiles.append((P, wraw[:, 6 * m + f, P * k:P * k + P]))
                    else:
                        f, d = n // 2, n % 2
                        down = wraw[:, 12:18, :].rearrange("p (t j) d -> p t (j d)", t=2)
                        tiles.append((P, down[:, d, P * f:P * f + P]))
                transposes(("wT", j), tiles)
            for j in range(7, 9):
                await_taken(pe, ("wT", j))
            scores(Seg(0), 0)
            scores(Seg(0), 1)

            def run(seg):
                t0 = seg.t0
                slots = dict(segment_jobs(t0))
                for st in range(ST):
                    if st + 2 < ST:
                        scores(seg, st + 2)
                    elif t0 + 1 < SEGS:
                        scores(seg.next(), st + 2 - ST)
                    key = slots.get(st)
                    if key is None:
                        pass
                    elif key[0] == "den":
                        den_job(seg, t0 - 1)
                    elif key[0] == "q":
                        q_job(seg, t0 + 1, loaded((t0 + 1) // NBS, seg))
                    elif key[0] == "k":
                        k_job(seg, key[1], key[2], loaded(key[1], seg))
                    elif key[0] == "v":
                        v_job(seg, key[1], key[2], loaded(key[1], seg))
                    else:
                        y_job(seg, t0 - 1, key[2])
                    values(seg, st)

            segments(pe, run)
            end = Seg(SEGS)
            den_job(end, SEGS - 1)
            y_job(end, SEGS - 1, 0)
            y_job(end, SEGS - 1, 1)

            def spread(n):
                pe.wait_ge(col_ready, n + 1)
                pe.transpose(ps[0:1, 7, 0:P], fsc[:, n, 0:1], ident[:, :]).then_inc(colT_ready, 1)
                pe.wait_ge(max_ready, n + 1)
                pe.matmul(ps[:, 7, 0:1], ones[0:1, :], frow[:, 0, 0:1], start=True, stop=True).then_inc(bc_ready, 1)

            await_taken(pe, ("y", SEGS - 1, 0))
            await_taken(pe, ("y", SEGS - 1, 1))
            for j in range(KT * NBS):
                k, b = j % KT, j // KT
                pe.wait_ge(h_norm, 4 * b + 4)
                if j == 4:
                    spread(0)
                if j >= 4:
                    pe.wait_ge(hT_done, j - 3)
                for i in range(4):
                    ins = pe.transpose(ps[:, j % 4, P * i:P * i + P], z[:, 4 * b + i, P * k:P * k + P], ident[:, :])
                ins.then_inc(hT_ready, 1)
            half = FT * NBS
            pe.wait_ge(hT_done, KT * NBS)
            pe.wait_ge(scale_done, 1)
            for c in range(2 * half):
                m, f, b = c // half, c // NBS % FT, c % NBS
                if c == half + 8:
                    pass
                if c >= 8:
                    pe.wait_ge(f1_out, c - 7)
                for k in range(KT):
                    ins = pe.matmul(ps[:, c % 8, :], wgu[:, m, k, P * f:P * f + P], hT[:, k, b * NB:(b + 1) * NB],
                                    start=(k == 0), stop=(k == KT - 1))
                ins.then_inc(f1_ready, 1)
                if c == half - 1:
                    pe.wait_ge(f1_out, half)
                    spread(1)
                    pe.wait_ge(scale_done, 2)
            pe.wait_ge(f1_out, 2 * half)
            spread(2)
            spread(3)
            spread(4)
            for g in range(NT // 2):
                if g % 2 == 0:
                    pe.wait_ge(oq_done, FT + g // 2 + 1)
                if g >= 4:
                    pe.wait_ge(f2_out, g - 3)
                for m in range(2):
                    n = 2 * g + m
                    for f in range(FT):
                        ins = pe.matmul(ps[:, g % 4, DM * m:DM * m + DM], up[:, f, P * n:P * n + P], wdT[:, f, :],
                                        start=(f == 0), stop=(f == FT - 1))
                ins.then_inc(f2_ready, 1)


_INS = ['x', 'ctx_1024', 'g_xattn', 'g_ffn', 'L0_xattn_ln_l_w', 'L0_xattn_ln_l_b', 'L0_xattn_ln_c_w', 'L0_xattn_ln_c_b',
        'L0_xattn_Wq', 'L0_xattn_Wkv', 'L0_xattn_Wo', 'L0_xattn_bo', 'L0_ffn_w_gate', 'L0_ffn_w_up', 'L0_ffn_w_down']


def kernel(**inputs):
    import numpy as _np
    import concourse.bacc as _bacc
    from concourse import mybir as _mybir
    from concourse.bass_utils import run_bass_kernel_spmd as _run

    nc = _bacc.Bacc("TRN2", target_bir_lowering=False, num_devices=1)
    arrays, args = {}, []
    for name in _INS:
        a = _np.ascontiguousarray(inputs[name])
        arrays[f"in_{name}_dram"] = a
        args.append(nc.dram_tensor(f"in_{name}_dram", a.shape, _mybir.dt.from_np(a.dtype), kind="ExternalInput").ap())
    args.append(nc.dram_tensor("out_0_dram", (1, N, DM), F32, kind="ExternalOutput").ap())
    attention_ffn(nc, *args)
    r = _run(nc, [arrays], core_ids=[0])
    return r.results[0]["out_0_dram"]
```

```python
from contextlib import ExitStack

import concourse.bass as bass
from concourse import mybir

ALU = mybir.AluOpType
ACT = mybir.ActivationFunctionType
AX_X = mybir.AxisListType.X
F32 = mybir.dt.float32
F32R = mybir.dt.float32r
I16 = mybir.dt.int16
I32 = mybir.dt.int32
U16T = mybir.dt.uint16

P = 128
N, S, DM = 2048, 1601, 256
H, DH = 16, 64
FF = 768
QB = 32
KT = DM // P
PAIRS = H // 2
NB = 512
NBS = N // NB
NT = N // P
ST = -(-S // P)
SLAST = S - (ST - 1) * P
SPAD = S + 1
SB = -(-S // NB)
SEGS = PAIRS * NBS
LOOP0, LOOPS, UNROLL = 1, 3, 8
TAIL0 = LOOP0 + LOOPS * UNROLL
WQ0, WT0 = TAIL0, SEGS - NBS
E_BUFS = 4
EPS = 1e-5
CLIP = 11.0
EXP_LO, EXP_HI = 1.6701700790245659e-05, 59874.14171519782
MAGIC = 12582912.0
QMAX = 32767.0
ROOT_MAGIC = 1597463007.0
NEWTON = 3
WMAX = 7.0
U16 = 65536.0
FT = FF // P
WBLK = FF // QB
FC = 2 * NB
FCH = FT * N // FC


def rows_of(st):
    return P if st < ST - 1 else SLAST


def cols_of(b):
    return min(NB, S - b * NB)


class Seg:

    def __init__(self, t0, i=None):
        self.t0, self.i = t0, i

    def count(self, per_segment, c):
        v = per_segment * self.t0 + c
        return v if self.i is None else v + per_segment * UNROLL * self.i

    def next(self):
        return Seg(self.t0 + 1, self.i)


def segment_jobs(t):
    if t == 0:
        return [(2, ("lT", 1, 0)), (2, ("lT", 1, 1)), (4, ("q", 1)), (5, ("lT", 2, 0)), (6, ("lT", 2, 1)),
                (7, ("k", 1, 0)), (9, ("lT", 3, 0)), (10, ("lT", 3, 1)), (11, ("v", 1, 0))]
    jobs = [(1, ("den", t - 1))]
    if t + 1 < SEGS:
        jobs.append((3, ("q", t + 1)))
    p = t // NBS + 1
    wm = t - WT0
    if p < PAIRS:
        jobs.append((6, ("k", p, t % NBS)))
    elif wm < 3:
        jobs += [(6, ("wT", wm, 0)), (7, ("wT", wm, 1))]
    jobs += [(8, ("y", t - 1, 0)), (10, ("y", t - 1, 1))]
    if p < PAIRS:
        jobs.append((11, ("v", p, t % NBS)))
    elif wm < 3:
        jobs.append((11, ("wT", wm, 2)))
    return jobs


def job_table():
    order = [("cT", b, k) for b in range(SB) for k in range(KT)]
    order += [("lT", 0, k) for k in range(KT)] + [("q", 0)]
    order += [("k", 0, b) for b in range(SB)] + [("v", 0, b) for b in range(SB)]
    for t in range(SEGS):
        order += [key for _, key in segment_jobs(t)]
    order += [("den", SEGS - 1), ("y", SEGS - 1, 0), ("y", SEGS - 1, 1)]
    return {key: n for n, key in enumerate(order)}


JOBS = job_table()
PER_LOOP = 6 * UNROLL // 2


def bank_of(key):
    return JOBS[key] % 2


def place_of(key, seg):
    n = JOBS[key] // 2
    return n if seg is None or seg.i is None else n + PER_LOOP * seg.i


def attention_ffn(nc, x, ctx_rows, g_xattn, g_ffn, ln_l_w, ln_l_b, ln_c_w, ln_c_b,
                  Wq, Wkv, Wo, bo, w_gate, w_up, w_down, out):
    with ExitStack() as ctx:
        def sb(name, shape, dt=F32, stack=ctx):
            return stack.enter_context(nc.sbuf_tensor(name, shape, dt))

        def sem(name):
            return ctx.enter_context(nc.semaphore(name))

        xacc = sb("xacc", [P, NT, DM])
        z = sb("z", [P, NT, DM])
        ident = sb("ident", [P, P])
        ones = sb("ones", [P, P])
        gates = sb("gates", [P, 2])
        tg = sb("tg", [P, 2])
        cols = sb("cols", [P, 4, KT])
        bo_t = sb("bo_t", [P, DM])
        stats = sb("stats", [P, 2, NT, 6])
        mv = sb("mv", [P, 3, NT, 2])
        lnt = sb("lnt", [P, 3, 3, NT])
        fst = sb("fst", [P, 5, 32])
        wdT = sb("wdT", [P, 2, FT, DM], F32R)
        with ExitStack() as early:
            kb_even = sb("kb_even", [P, 2, 2, SPAD], F32R, stack=early)
        wgu = sb("wgu", [P, 2, 2, KT, FF], F32R)
        sb("pad", [P, 2 * 2 * SPAD - 4 * KT * FF])

        with ExitStack() as att:
            latT = sb("latT", [P, KT, N], stack=att)
            ctxT = sb("ctxT", [P, KT, S], stack=att)
            vb = sb("vb", [P, 2, ST, P], stack=att)
            qb = sb("qb", [P, 2, 2, NB], F32R, stack=att)
            e_buf = sb("e_buf", [P, E_BUFS, 2, NB], stack=att)
            acc = sb("acc", [P, 2, 2, NB], stack=att)
            rden = sb("rden", [P, NB], stack=att)
            oT = sb("oT", [P, 2, NB], stack=att)
            wst = sb("wst", [P, 2, 3, KT, P], stack=att)
            wo_raw = sb("wo_raw", [P, 2, DM], stack=att)
            wo_g = sb("wo_g", [P, 2, DM], stack=att)
            wdown1 = sb("wdown1", [P, FF], stack=att)
            wsc = sb("wsc", [P, 6, 3, WBLK], stack=att)
            kb = (kb_even, sb("kb_odd", [P, 2, 2, SPAD], F32R, stack=att))
            e_flat = e_buf[:, :, :, :].rearrange("p a b n -> p (a b n)")
            crow = e_flat[:, 0:ST * DM].rearrange("p (t d) -> p t d", d=DM)

        with ExitStack() as ffn:
            fsc = sb("fsc", [P, 5, 4], stack=ffn)
            frow = sb("frow", [1, 5, 4], stack=ffn)
            pre = sb("pre", [1, 2], stack=ffn)
            gt = sb("gt", [P, FT, N], stack=ffn)
            with ExitStack() as first:
                hT = sb("hT", [P, 2, KT, N], F32R, stack=first)
                up = sb("up", [P, FT, N], stack=first)
            ui = sb("ui", [P, FT, N], I16, stack=ffn)
            sb("pad2", [P, (2 * KT * N - FT * N // 2)], stack=ffn)
            ohl = sb("ohl", [P, 2, 2, FT, DM], F32R, stack=ffn)
            oi = sb("oi", [P, 2, FT, DM], I16, stack=ffn)
        zf = z[:, :, :].rearrange("p t d -> p (t d)")
        hi16 = zf[:, 0:N].bitcast(I16)
        sg = zf[:, 0:2 * FC].rearrange("p (a n) -> p a n", a=2)
        gi = zf[:, 2 * FC:3 * FC].bitcast(I16).rearrange("p (a n) -> p a n", a=2)
        su = zf[:, 3 * FC:4 * FC].bitcast(U16T).rearrange("p (a n) -> p a n", a=2)
        wpiece = [zf[:, FF * n:FF * n + FF] for n in range(5)] + [wdown1[:, :]]

        psum = nc.psum_tensor("ps", [P, 8, NB], F32)
        ps = ctx.enter_context(psum)
        ps_s, ps_o, ps_m = ps[:, 0:4, :], ps[:, 4:6, :], ps[:, 6:8, :]
        sc = ps_s.rearrange("p (a h) n -> p a h n", h=2)

        in_ctx, in_x = [sem(f"in_ctx{b}") for b in range(SB)], [sem(f"in_x{b}") for b in range(NBS)]
        in_small, in_w = sem("in_small"), sem("in_w")
        w_loaded = [sem("w_loaded0"), sem("w_loaded1")]
        ident_zero, ident_done, const_done = sem("ident_zero"), sem("ident_done"), sem("const_done")
        dve_chain = sem("dve_chain")
        ctx_norm, lat_norm = sem("ctx_norm"), sem("lat_norm")
        w_inverse, w_scaled, w_round, w_quant = sem("w_inverse"), sem("w_scaled"), sem("w_round"), sem("w_quant")
        tanh_done, wo_scaled, bias_added, bias_scaled = sem("tanh_done"), sem("wo_scaled"), sem("bias_added"), sem("bias_scaled")
        job_ready = [sem("job_ready0"), sem("job_ready1")]
        job_taken = [sem("job_taken0"), sem("job_taken1")]
        q_high, k_high, w_high = sem("q_high"), sem("k_high"), sem("w_high")
        scores_ready, exp_done, clip_done, pv_done = sem("scores_ready"), sem("exp_done"), sem("clip_done"), sem("pv_done")
        sum_a, sum_b = sem("sum_a"), sem("sum_b")
        norm_done = sem("norm_done")
        h_norm, h_top, hT_ready, h_int, h_high, h_low = sem("h_norm"), sem("h_top"), sem("hT_ready"), sem("h_int"), sem("h_high"), sem("h_low")
        col_ready, colT_ready, max_ready, bc_ready = sem("col_ready"), sem("colT_ready"), sem("max_ready"), sem("bc_ready")
        scale_done = sem("scale_done")
        f1_ready, f1_out = sem("f1_ready"), sem("f1_out")
        gi_done, sig_done, su_done = sem("gi_done"), sem("sig_done"), sem("su_done")
        gs_done, gq_done, ui_done, ui_pool, o_done = sem("gs_done"), sem("gq_done"), sem("ui_done"), sem("ui_pool"), sem("o_done")
        oi_done, o_high, o_low = sem("oi_done"), sem("o_high"), sem("o_low")
        f2_ready, f2_out, stored = sem("f2_ready"), sem("f2_out"), sem("stored")

        block = ctx.enter_context(nc.Block())

        def await_job(eng, key, seg=None):
            eng.wait_ge(job_ready[bank_of(key)], place_of(key, seg) + 1)

        def await_taken(eng, key, seg=None):
            eng.wait_ge(job_taken[bank_of(key)], place_of(key, seg) + 1)

        def await_all_taken(eng, keys, seg=None):
            for bank in range(2):
                mine = [key for key in keys if bank_of(key) == bank]
                if mine:
                    await_taken(eng, max(mine, key=JOBS.get), seg)

        def segments(eng, run):
            run(Seg(0))
            with eng.Fori(0, LOOPS) as i:
                for t0 in range(LOOP0, LOOP0 + UNROLL):
                    run(Seg(t0, i))
            for t in range(TAIL0, SEGS):
                run(Seg(t))

        def chunk(a, e):
            return a[:, e // 2, FC * (e % 2):FC * (e % 2) + FC]

        def w_at(m, part, j):
            if m == 2:
                return wdT[:, part, :, :].rearrange("p f d -> p (f d)")[:, j * NB:(j + 1) * NB]
            return wgu[:, m, part, :, :].rearrange("p k f -> p (k f)")[:, j * NB:(j + 1) * NB]

        def await_ui(eng, e):
            eng.wait_ge((ui_pool, ui_done)[e % 2], e // 2 + 1)

        @block.sync
        def _(sp):
            for b in range(SB - 1):
                sp.dma_start(crow[:, 4 * b:4 * b + 4, :],
                             ctx_rows[0, b * NB:(b + 1) * NB, :].rearrange("(t p) d -> p t d", p=P)).then_inc(in_ctx[b], 16)
            sp.dma_start(crow[0:SLAST, ST - 1, :], ctx_rows[0, (ST - 1) * P:S, :]).then_inc(in_ctx[SB - 1], 16)

            def load_x(b):
                sp.dma_start(xacc[:, 4 * b:4 * b + 4, :],
                             x[0, b * NB:(b + 1) * NB, :].rearrange("(t p) d -> p t d", p=P)).then_inc(in_x[b], 16)

            load_x(0)
            for n, a in enumerate((ln_l_w, ln_l_b, ln_c_w, ln_c_b)):
                sp.dma_start(cols[:, n, :], a.rearrange("(k p) -> p k", k=KT), allow_slow_non_contiguous=True).then_inc(in_small, 16)
            for n, a in enumerate((g_xattn, g_ffn)):
                sp.dma_start(gates[:, n:n + 1], a.rearrange("(a n) -> a n", a=1).to_broadcast([P, 1])).then_inc(in_small, 16)
            sp.dma_start(bo_t[:, :], bo.rearrange("(a n) -> a n", a=1).to_broadcast([P, DM])).then_inc(in_small, 16)

            def load_pair(p, parity):
                for n, (w, at) in enumerate(((Wq, 0), (Wkv, 0), (Wkv, H * DH))):
                    sp.dma_start(wst[:, parity, n, :, :],
                                 w[:, bass.ds(P * p + at, P)].rearrange("(k q) n -> q k n", q=P)).then_inc(w_loaded[parity], 16)
                sp.dma_start(wo_raw[:, parity, :], Wo[bass.ds(P * p, P), :]).then_inc(w_loaded[parity], 16)

            load_pair(0, 0)
            for b in range(1, NBS):
                load_x(b)
            load_pair(1, 1)

            def run(seg):
                if seg.t0 % NBS != NBS - 1 or (seg.t0 + 5) // NBS >= PAIRS:
                    return
                p = (seg.t0 + 5) // NBS
                await_taken(sp, ("q", seg.t0), seg)
                sp.wait_ge(wo_scaled, p - 1 if seg.i is None else p - 1 + 2 * seg.i)
                load_pair(p if seg.i is None else p + 2 * seg.i, p % 2)

            segments(sp, run)
            await_taken(sp, ("lT", NBS - 1, 1))
            for n, w in enumerate((w_gate, w_up)):
                sp.dma_start(zf[:, n * FT * DM:(n + 1) * FT * DM].rearrange("p (t d) -> p t d", d=DM),
                             w.rearrange("(t p) d -> p t d", p=P)).then_inc(in_w, 16)
            for n in range(KT):
                sp.dma_start(wpiece[4 + n], w_down[P * n:P * n + P, :]).then_inc(in_w, 16)
            for g in range(NT // 2):
                sp.wait_ge(f2_out, g + 1)
                sp.dma_start(out[0, 2 * g * P:(2 * g + 2) * P, :].rearrange("(t p) d -> p t d", p=P),
                             z[:, 2 * g:2 * g + 2, :]).then_inc(stored, 16)
            sp.wait_ge(stored, 16 * (NT // 2))

        @block.gpsimd
        def _(pool):
            pool.memset(ident[:, :], 0.0).then_inc(ident_zero, 1)
            pool.wait_ge(ident_zero, 1)
            pool.affine_select(out=ident[:, :], in_=ident[:, :], compare_op=ALU.not_equal, fill=1.0, base=0,
                               pattern=[[-1, P]], channel_multiplier=1).then_inc(ident_done, 1)
            pool.wait_ge(tanh_done, 1)
            pool.wait_ge(in_small, 16 * 7)
            pool.tensor_scalar(bo_t[:, :], bo_t[:, :], tg[:, 0:1], None, ALU.mult).then_inc(bias_scaled, 1)
            pool.wait_ge(bias_scaled, 1)

            def run(seg):
                t0 = seg.t0
                if t0 % NBS == 0:
                    p = t0 // NBS
                    pool.wait_ge(w_loaded[p % 2], (p // 2 + 1) * 64 if seg.i is None else (p // 2 + 1) * 64 + 64 * seg.i)
                    if t0 > NBS:
                        await_job(pool, ("y", t0 - NBS - 1, 1), seg)
                    pool.tensor_tensor(wo_g[:, p % 2, :], wo_raw[:, p % 2, :], tg[:, 0:1].to_broadcast([P, DM]),
                                       ALU.mult).then_inc(wo_scaled, 1)
                for st in range(1, ST):
                    r = rows_of(st)
                    pool.wait_ge(clip_done, seg.count(ST, st + 1))
                    if st == 1:
                        if t0 >= 2:
                            await_job(pool, ("den", t0 - 2), seg)
                        a = e_buf[:, (ST * t0) % E_BUFS, 1, :]
                    else:
                        pool.wait_ge(sum_b, seg.count(ST - 1, st - 1))
                        a = acc[0:r, t0 % 2, 1, :]
                    pool.tensor_tensor(acc[0:r, t0 % 2, 1, :], a, e_buf[0:r, (ST * t0 + st) % E_BUFS, 1, :],
                                       ALU.add).then_inc(sum_b, 1)
                    if t0 == 0 and st % 3 == 0:
                        b = st // 3 - 1
                        pool.wait_ge(lat_norm, 4 * b + 4)
                        for i in range(4):
                            pool.tensor_tensor(xacc[:, 4 * b + i, :], xacc[:, 4 * b + i, :], bo_t[:, :], ALU.add).then_inc(bias_added, 1)

                    n, at = divmod(st, 6)
                    if WQ0 <= t0 < WT0 and at in (2, 5) and n < 2:
                        w = 2 * (t0 - WQ0) + (0 if at == 2 else 1)
                        blocks = wpiece[w].rearrange("p (n e) -> p n e", e=QB)
                        by = wsc[:, w, 2 - n, :].unsqueeze(2).to_broadcast([P, WBLK, QB])
                        pool.wait_ge((w_inverse, w_round)[n], w + 1)
                        pool.tensor_tensor(blocks, blocks, by, ALU.mult).then_inc((w_scaled, w_quant)[n], 1)

            segments(pool, run)

            for e in range(FCH):
                pool.wait_ge(sig_done, e + 1)
                if e >= 2:
                    pool.wait_ge(gs_done, e - 1)
                pool.tensor_scalar(su[:, e % 2, :], sg[:, e % 2, :], U16, 1.0, ALU.mult, ALU.mult).then_inc(su_done, 1)
            pool.wait_ge(scale_done, 4)
            for e in range(0, FCH, 2):
                pool.tensor_scalar(chunk(ui, e), chunk(up, e), fsc[:, 2, 2:3], 1.0, ALU.mult, ALU.mult).then_inc(ui_pool, 1)

        @block.scalar
        def _(act):
            act.wait_ge(in_small, 16 * 7)
            nc.scalar.activation(tg[:, :], gates[:, :], ACT.Tanh).then_inc(tanh_done, 1)

            def take_T(key, dst, n, w):
                k = key[2]
                await_job(act, key)
                nc.scalar.activation(dst[:, k, key[1] * NB:key[1] * NB + w], ps_m[:, bank_of(key), 0:w], ACT.Identity,
                                     bias=cols[:, n + 1, k:k + 1], scale=cols[:, n, k:k + 1]).then_inc(job_taken[bank_of(key)], 1)

            def q_take(seg, t):
                await_job(act, ("q", t), seg)
                for h in range(2):
                    nc.scalar.copy(qb[0:DH, t % 2, h, :], ps_m[DH * h:DH * h + DH, bank_of(("q", t)), :]).then_inc(q_high, 1)

            def k_take(seg, p, b):
                w = cols_of(b)
                await_job(act, ("k", p, b), seg)
                for h in range(2):
                    for half in range(2):
                        nc.scalar.copy(kb[p % 2][DH * half:DH * half + DH, h, 0, b * NB:b * NB + w],
                                       ps_m[DH * h:DH * h + DH, bank_of(("k", p, b)), 0:w]).then_inc(k_high, 1)

            def v_take(seg, p, b):
                key = ("v", p, b)
                await_job(act, key, seg)
                if b < SB - 1:
                    nc.scalar.copy(vb[:, p % 2, 4 * b:4 * b + 4, :],
                                   ps_m[:, bank_of(key), :].rearrange("p (t n) -> p t n", n=P)).then_inc(job_taken[bank_of(key)], 1)
                else:
                    nc.scalar.copy(vb[0:SLAST, p % 2, ST - 1, :], ps_m[0:SLAST, bank_of(key), 0:P]).then_inc(job_taken[bank_of(key)], 1)

            for b in range(SB):
                for k in range(KT):
                    take_T(("cT", b, k), ctxT, 2, cols_of(b))
            for k in range(KT):
                take_T(("lT", 0, k), latT, 0, NB)
            q_take(None, 0)
            for b in range(SB):
                k_take(None, 0, b)
            for b in range(SB):
                v_take(None, 0, b)

            def w_take(m, j):
                key = ("wT", m, j)
                await_job(act, key)
                nc.scalar.copy(w_at(m, 0, j), ps_m[:, bank_of(key), :]).then_inc(w_high, 1)

            def run(seg):
                t0 = seg.t0
                for st in range(ST):
                    r, g = rows_of(st), ST * t0 + st
                    act.wait_ge(scores_ready, seg.count(ST, st + 1))
                    if g >= E_BUFS:
                        act.wait_ge(pv_done, seg.count(ST, st + 1 - E_BUFS))
                        back = Seg(t0 if st >= E_BUFS else t0 - 1, seg.i)
                        s0 = max((st - E_BUFS) % ST, 1)
                        act.wait_ge(sum_a, back.count(ST - 1, s0))
                        act.wait_ge(sum_b, back.count(ST - 1, s0))
                    nc.scalar.activation(e_buf[0:r, g % E_BUFS, :, :], sc[0:r, g % 2, :, :], ACT.Exp,
                                         scale=float(DH) ** -0.5).then_inc(exp_done, 1)
                    p = t0 // NBS + 1
                    if t0 == 0:
                        for b, k in {3: [(1, 0)], 4: [(1, 1)], 7: [(2, 0)], 8: [(2, 1)], 11: [(3, 0)], 12: [(3, 1)]}.get(st, []):
                            take_T(("lT", b, k), latT, 0, NB)
                    if st == 5 and t0 + 1 < SEGS:
                        q_take(seg, t0 + 1)
                    if WT0 <= t0 < WT0 + 3 and st in (8, 9, 12):
                        w_take(t0 - WT0, (8, 9, 12).index(st))
                    if st == (9 if t0 == 0 else 8) and p < PAIRS:
                        k_take(seg, p, t0 % NBS)
                    if st == 12 and p < PAIRS:
                        v_take(seg, p, t0 % NBS)

            segments(act, run)

            for j in range(KT * NBS):
                k, b = j % KT, j // KT
                piece = hi16[:, j * NB:(j + 1) * NB]
                act.wait_ge(hT_ready, max(j, 6) + 1)
                if j == 0:
                    act.wait_ge(scale_done, 1)
                nc.scalar.activation(piece, ps[:, j, :], ACT.Copy, scale=fsc[:, 0, 2:3]).then_inc(h_int, 1)
                act.wait_ge(h_int, j + 1)
                nc.scalar.copy(hT[:, 0, k, b * NB:(b + 1) * NB], piece).then_inc(h_high, 1)
            half = FT * NBS

            def f1_take(c):
                m, f, b = c // half, c // NBS % FT, c % NBS
                act.wait_ge(f1_ready, c + 1)
                nc.scalar.copy((gt, up)[m][:, f, b * NB:(b + 1) * NB], ps[:, c % 7, :]).then_inc(f1_out, 1)

            for c in range(half):
                f1_take(c)
            for e in range(FCH):
                f1_take(half + 2 * e)
                f1_take(half + 2 * e + 1)
                if e == 0:
                    act.wait_ge(scale_done, 2)
                    act.wait_ge(h_low, KT * NBS)
                if e >= 2:
                    act.wait_ge(su_done, e - 1)
                    act.wait_ge(gs_done, e - 1)
                nc.scalar.activation(gi[:, e % 2, :], chunk(gt, e), ACT.Copy, scale=fsc[:, 1, 2:3]).then_inc(gi_done, 1)
                act.wait_ge(gi_done, e + 1)
                nc.scalar.activation(sg[:, e % 2, :], gi[:, e % 2, :], ACT.Sigmoid, scale=fsc[:, 1, 1:2]).then_inc(sig_done, 1)
            act.wait_ge(scale_done, 4)
            for e in range(FCH):
                if e >= 2:
                    act.wait_ge(o_done, e - 1)
                nc.scalar.activation(gi[:, e % 2, :], chunk(gt, e), ACT.Copy, scale=fsc[:, 3, 2:3]).then_inc(gq_done, 1)
                if e % 2:
                    nc.scalar.activation(chunk(ui, e), chunk(up, e), ACT.Copy, scale=fsc[:, 2, 2:3]).then_inc(ui_done, 1)
            for g in range(NT // 2):
                act.wait_ge(oi_done, g + 1)
                if g >= 2:
                    act.wait_ge(f2_ready, g - 1)
                nc.scalar.copy(ohl[:, g % 2, 0, :, :], oi[:, g % 2, :, :]).then_inc(o_high, 1)

        @block.vector
        def _(dve):
            chain = [0]

            def link(ins):
                chain[0] += 1
                ins.then_inc(dve_chain, 1)
                dve.wait_ge(dve_chain, chain[0])

            def layernorm(n, tiles, src, dst, c1, c0, done):
                r = src[0].shape[0]
                first, w = tiles[0], len(tiles)
                for t, a in zip(tiles, src):
                    ins = dve.bn_stats(stats[0:r, n % 2, t, :], a)
                link(ins)
                for t in tiles:
                    ins = dve.bn_aggr(mv[0:r, n, t, :], stats[0:r, n % 2, t, :])
                link(ins)
                a, y, u = (lnt[0:r, n, j, first:first + w] for j in range(3))
                link(dve.tensor_scalar(a, mv[0:r, n, first:first + w, 1], c1, c0, ALU.mult, ALU.add))
                link(dve.tensor_scalar(y.bitcast(I32), a.bitcast(I32), 1, None, ALU.logical_shift_right))
                link(dve.tensor_scalar(y.bitcast(I32), y.bitcast(I32), -1.0, ROOT_MAGIC, ALU.mult, ALU.add))
                for _ in range(NEWTON):
                    link(dve.tensor_tensor(u, y, y, ALU.mult))
                    link(dve.scalar_tensor_tensor(out=u, in0=u, scalar=-0.5, in1=a, op0=ALU.mult, op1=ALU.mult))
                    link(dve.scalar_tensor_tensor(out=y, in0=u, scalar=1.5, in1=y, op0=ALU.add, op1=ALU.mult))
                for t, a, b in zip(tiles, src, dst):
                    dve.tensor_scalar(b, a, mv[0:r, n, t, 0:1], lnt[0:r, n, 1, t:t + 1], ALU.subtract, ALU.mult).then_inc(done, 1)

            def context_norm(b):
                tiles = range(4 * b, min(4 * b + 4, ST))
                rows = [crow[0:rows_of(t), t, :] for t in tiles]
                dve.wait_ge(in_ctx[b], 16)
                layernorm(0, tiles, rows, rows, 1.0, EPS, ctx_norm)

            def latent_norm(b):
                tiles = range(4 * b, 4 * b + 4)
                dve.wait_ge(in_x[b], 16)
                layernorm(1, tiles, [xacc[:, t, :] for t in tiles], [z[:, t, :] for t in tiles], 1.0 + EPS, EPS * EPS, lat_norm)

            def top(dst, src):
                return dve.tensor_reduce(dst, src, AX_X, ALU.max, apply_absolute_value=True)

            def ffn_norm(b):
                tiles = range(4 * b, 4 * b + 4)
                layernorm(2, tiles, [xacc[:, t, :] for t in tiles], [z[:, t, :] for t in tiles], 1.0, EPS, h_norm)
                dve.wait_ge(h_norm, 4 * b + 4)
                top(fst[:, 0, b:b + 1], z[:, 4 * b:4 * b + 4, :].rearrange("p t d -> p (t d)")).then_inc(h_top, 1)

            dve.memset(ones[:, :], 1.0).then_inc(const_done, 1)
            for b in range(SB):
                context_norm(b)
            latent_norm(0)

            def q_low(seg, t):
                bank = bank_of(("q", t))
                for h in range(2):
                    dve.wait_ge(q_high, 2 * (t if seg is None else seg.t0 + 1) + 1 + h + (0 if seg is None or seg.i is None else 2 * UNROLL * seg.i))
                    ins = dve.tensor_tensor(qb[DH:P, t % 2, h, :], ps_m[DH * h:DH * h + DH, bank, :],
                                            qb[0:DH, t % 2, h, :].bitcast(F32), ALU.subtract)
                ins.then_inc(job_taken[bank], 1)

            def k_low(seg, p, b, h):
                w, bank = cols_of(b), bank_of(("k", p, b))
                done = 4 * (b + (p * NBS if seg is None else seg.t0 - seg.t0 % NBS + NBS)) + 2 * h + 2
                dve.wait_ge(k_high, done + (0 if seg is None or seg.i is None else 4 * UNROLL * seg.i))
                for half in range(2):
                    lo, hi = DH * half, DH * half + DH
                    ins = dve.tensor_tensor(kb[p % 2][lo:hi, h, 1, b * NB:b * NB + w], ps_m[DH * h:DH * h + DH, bank, 0:w],
                                            kb[p % 2][lo:hi, h, 0, b * NB:b * NB + w].bitcast(F32), ALU.subtract)
                if h == 1:
                    ins.then_inc(job_taken[bank], 1)

            q_low(None, 0)
            for b in range(SB):
                for h in range(2):
                    k_low(None, 0, b, h)

            def w_scales(w):
                blocks = wpiece[w].rearrange("p (n e) -> p n e", e=QB)
                dve.wait_ge(in_w, 64)
                link(top(wsc[:, w, 0, :], blocks))
                link(dve.tensor_scalar(wsc[:, w, 1, :], wsc[:, w, 0, :], 1.0 / WMAX, 1e-12, ALU.mult, ALU.max))
                dve.reciprocal(wsc[:, w, 2, :], wsc[:, w, 1, :]).then_inc(w_inverse, 1)

            def w_integers(w):
                dve.wait_ge(w_scaled, w + 1)
                dve.tensor_scalar(wpiece[w], wpiece[w], MAGIC, MAGIC, ALU.add, ALU.subtract).then_inc(w_round, 1)

            def w_low(m, j):
                key = ("wT", m, j)
                dve.wait_ge(w_high, 3 * m + j + 1)
                dve.tensor_tensor(w_at(m, 1, j), ps_m[:, bank_of(key), :], w_at(m, 0, j).bitcast(F32),
                                  ALU.subtract).then_inc(job_taken[bank_of(key)], 1)

            def add_a(seg, st):
                t0, r = seg.t0, rows_of(st)
                if st == 1:
                    a = e_buf[:, (ST * t0) % E_BUFS, 0, :]
                else:
                    a = acc[0:r, t0 % 2, 0, :]
                    dve.wait_ge(sum_a, seg.count(ST - 1, st - 1))
                dve.wait_ge(clip_done, seg.count(ST, st + 1))
                dve.tensor_tensor(acc[0:r, t0 % 2, 0, :], a, e_buf[0:r, (ST * t0 + st) % E_BUFS, 0, :],
                                  ALU.add).then_inc(sum_a, 1)

            def invert(seg, t, c):
                bank, w = bank_of(("den", t)), NB // 4
                await_job(dve, ("den", t), seg)
                ins = dve.reciprocal(rden[:, c * w:(c + 1) * w], ps_m[:, bank, c * w:(c + 1) * w])
                if c == 3:
                    ins.then_inc(job_taken[bank], 1)

            def scale_out(seg, t):
                await_taken(dve, ("den", t), seg)
                dve.wait_ge(pv_done, Seg(t, seg.i).count(ST, ST))
                dve.tensor_tensor(oT[:, t % 2, :], ps_o[:, t % 2, :], rden[:, :], ALU.mult).then_inc(norm_done, 1)

            def add_y(seg, t, half):
                key = ("y", t, half)
                n0 = 4 * (t % NBS) + 2 * half
                await_job(dve, key, seg)
                if seg.t0 <= 4:
                    dve.wait_ge(bias_added, NT)
                dst = xacc[:, n0:n0 + 2, :]
                dve.tensor_tensor(dst, ps_m[:, bank_of(key), :].rearrange("p (t d) -> p t d", d=DM), dst,
                                  ALU.add).then_inc(job_taken[bank_of(key)], 1)

            def run(seg):
                t0 = seg.t0
                p = t0 // NBS + 1
                for st in range(ST):
                    r, g = rows_of(st), ST * t0 + st
                    dve.wait_ge(exp_done, seg.count(ST, st + 1))
                    tile = e_buf[0:r, g % E_BUFS, :, :]
                    dve.tensor_scalar(tile, tile, EXP_LO, EXP_HI, ALU.max, ALU.min).then_inc(clip_done, 1)
                    if st >= 2:
                        add_a(seg, st - 1)
                    elif st == 0 and t0 >= 1:
                        add_a(Seg(t0 - 1, seg.i), ST - 1)
                    if t0 >= 1 and 3 <= st <= 6:
                        invert(seg, t0 - 1, st - 3)
                    if st == 7 and t0 >= 1:
                        scale_out(seg, t0 - 1)
                    if t0 == 0 and st in (0, 3, 7):
                        latent_norm(1 + st // 3)
                    if st == (6 if t0 == 0 else 8) and t0 + 1 < SEGS:
                        q_low(seg, t0 + 1)
                    k_step = 10 if t0 == 0 else 9
                    if k_step <= st < k_step + 2 and p < PAIRS:
                        k_low(seg, p, t0 % NBS, st - k_step)
                    if WQ0 <= t0 < WT0:
                        w = 2 * (t0 - WQ0)
                        if st < 2:
                            w_scales(w + st)
                        if st in (7, 11):
                            w_integers(w + st // 11)
                    if WT0 <= t0 < WT0 + 3 and st in (9, 10):
                        w_low(t0 - WT0, st - 9)
                    if st == 10 and t0 >= 1:
                        add_y(seg, t0 - 1, 0)
                    if st == 12 and t0 >= 1:
                        add_y(seg, t0 - 1, 1)
                    if WT0 <= t0 < WT0 + 3 and st == 12:
                        w_low(t0 - WT0, 2)
                    if t0 >= SEGS - 2 and st == 0:
                        await_taken(dve, ("y", SEGS - NBS + t0 - (SEGS - 2), 1))
                        ffn_norm(t0 - (SEGS - 2))

            segments(dve, run)
            end = Seg(SEGS)
            add_a(Seg(SEGS - 1), ST - 1)
            for c in range(4):
                invert(end, SEGS - 1, c)
            scale_out(end, SEGS - 1)
            await_taken(dve, ("y", SEGS - 2, 1))
            await_taken(dve, ("y", SEGS - 2, 0))
            ffn_norm(2)
            add_y(end, SEGS - 1, 0)
            add_y(end, SEGS - 1, 1)
            await_taken(dve, ("y", SEGS - 1, 0))
            await_taken(dve, ("y", SEGS - 1, 1))
            ffn_norm(3)

            def scale_of(n, pieces, pre):
                top(fsc[:, n, 0:1], fst[:, n, 0:pieces]).then_inc(col_ready, 1)
                dve.wait_ge(colT_ready, n + 1)
                link(top(frow[:, n, 0:1], ps[0:1, 7, 0:P]))
                link(dve.scalar_tensor_tensor(out=frow[:, n, 1:2], in0=frow[:, n, 0:1], scalar=1.0 / QMAX, in1=pre,
                                              op0=ALU.mult, op1=ALU.mult))
                link(dve.tensor_scalar(frow[:, n, 2:3], frow[:, n, 1:2], 1e-12, None, ALU.max))
                link(dve.reciprocal(frow[:, n, 3:4], frow[:, n, 2:3]))
                dve.tensor_tensor(frow[:, n, 3:4], frow[:, n, 3:4], pre, ALU.mult).then_inc(max_ready, 1)
                dve.wait_ge(bc_ready, n + 1)
                dve.tensor_copy(fsc[:, n, 1:3], ps[:, 7, 0:2]).then_inc(scale_done, 1)
                dve.wait_ge(scale_done, n + 1)

            dve.wait_ge(h_top, NBS)
            scale_of(0, NBS, ones[0:1, 0:1])
            for j in range(KT * NBS):
                k, b = j % KT, j // KT
                dve.wait_ge(h_high, j + 1)
                dve.tensor_tensor(hT[:, 1, k, b * NB:(b + 1) * NB], hi16[:, j * NB:(j + 1) * NB],
                                  hT[:, 0, k, b * NB:(b + 1) * NB].bitcast(F32), ALU.subtract).then_inc(h_low, 1)
            half = FT * NBS

            def f1_top(m, c):
                dve.wait_ge(f1_out, half * m + c + 1)
                return top(fst[:, 1 + m, c:c + 1], (gt, up)[m][:, c // NBS, c % NBS * NB:(c % NBS + 1) * NB])

            for c in range(half):
                ins = f1_top(0, c)
            link(ins)
            x_scale = frow[:, 0, 2:3]
            scale_of(1, half, x_scale)
            link(dve.tensor_scalar(pre[:, 0:1], frow[:, 1, 2:3], 1.0 / U16, None, ALU.mult))
            for e in range(FCH):
                f1_top(1, 2 * e)
                up_top = f1_top(1, 2 * e + 1)
                if e == FCH - 1:
                    link(up_top)
                dve.wait_ge(su_done, e + 1)
                dve.tensor_tensor(chunk(gt, e), gi[:, e % 2, :], su[:, e % 2, :], ALU.mult).then_inc(gs_done, 1)
                if e >= 1:
                    dve.wait_ge(gs_done, e)
                    top(fst[:, 3, e - 1:e], chunk(gt, e - 1))
            scale_of(2, half, x_scale)
            dve.wait_ge(gs_done, FCH)
            link(top(fst[:, 3, FCH - 1:FCH], chunk(gt, FCH - 1)))
            scale_of(3, FCH, pre[:, 0:1])
            link(dve.tensor_tensor(pre[:, 1:2], frow[:, 3, 2:3], frow[:, 2, 2:3], ALU.mult))
            for e in range(FCH):
                dve.wait_ge(gq_done, e + 1)
                await_ui(dve, e)
                dve.tensor_tensor(chunk(gt, e), gi[:, e % 2, :], chunk(ui, e), ALU.mult).then_inc(o_done, 1)
                if e >= 1:
                    dve.wait_ge(o_done, e)
                    top(fst[:, 4, e - 1:e], chunk(gt, e - 1))
            dve.wait_ge(o_done, FCH)
            link(top(fst[:, 4, FCH - 1:FCH], chunk(gt, FCH - 1)))
            scale_of(4, FCH, pre[:, 1:2])
            link(dve.tensor_tensor(fsc[:, 4, 3:4], fsc[:, 4, 1:2], tg[:, 1:2], ALU.mult))

            def out_integers(g):
                if g >= 2:
                    dve.wait_ge(o_high, g - 1)
                    dve.wait_ge(o_low, g - 1)
                dve.tensor_scalar(oi[:, g % 2, :, :], gt[:, :, DM * g:DM * g + DM], fsc[:, 4, 2:3], None,
                                  ALU.mult).then_inc(oi_done, 1)

            def out_low(g):
                dve.wait_ge(o_high, g + 1)
                dve.wait_ge(oi_done, g + 1)
                dve.tensor_tensor(ohl[:, g % 2, 1, :, :], oi[:, g % 2, :, :], ohl[:, g % 2, 0, :, :].bitcast(F32),
                                  ALU.subtract).then_inc(o_low, 1)

            def result(g):
                dve.wait_ge(f2_ready, g + 1)
                dve.scalar_tensor_tensor(out=z[:, 2 * g:2 * g + 2, :], in0=ps[:, g % 4, :].rearrange("p (t d) -> p t d", d=DM),
                                         scalar=fsc[:, 4, 3:4], in1=xacc[:, 2 * g:2 * g + 2, :],
                                         op0=ALU.mult, op1=ALU.add).then_inc(f2_out, 1)

            out_integers(0)
            for g in range(NT // 2):
                if g + 1 < NT // 2:
                    out_integers(g + 1)
                out_low(g)
                if g >= 2:
                    result(g - 2)
            result(NT // 2 - 2)
            result(NT // 2 - 1)

        @block.tensor
        def _(pe):
            def bank_free(key, seg=None):
                n = place_of(key, seg)
                if JOBS[key] >= 2:
                    pe.wait_ge(job_taken[bank_of(key)], n)
                return ps_m[:, bank_of(key), :]

            def transposes(key, tiles):
                bank = bank_free(key)
                for i, (r, src) in enumerate(tiles):
                    ins = pe.transpose(bank[:, P * i:P * i + r], src, ident[0:r, 0:r])
                ins.then_inc(job_ready[bank_of(key)], 1)

            def q_job(seg, t, at):
                bank = bank_free(("q", t), seg)
                pe.wait_ge(w_loaded[at[0]], at[1])
                b = t % NBS
                if t < NBS:
                    await_all_taken(pe, [("lT", b, k) for k in range(KT)])
                for k in range(KT):
                    ins = pe.matmul(bank, wst[:, at[0], 0, k, :], latT[:, k, b * NB:(b + 1) * NB], start=(k == 0), stop=(k == KT - 1))
                ins.then_inc(job_ready[bank_of(("q", t))], 1)

            def k_job(seg, p, b, at):
                key, w = ("k", p, b), cols_of(b)
                bank = bank_free(key, seg)
                pe.wait_ge(w_loaded[at[0]], at[1])
                for k in range(KT):
                    ins = pe.matmul(bank[:, 0:w], wst[:, at[0], 1, k, :], ctxT[:, k, b * NB:b * NB + w], start=(k == 0), stop=(k == KT - 1))
                ins.then_inc(job_ready[bank_of(key)], 1)

            def v_job(seg, p, b, at):
                key = ("v", p, b)
                bank = bank_free(key, seg)
                for i, st in enumerate(range(4 * b, min(4 * b + 4, ST))):
                    r = rows_of(st)
                    for k in range(KT):
                        ins = pe.matmul(bank[0:r, P * i:P * i + P], ctxT[:, k, P * st:P * st + r], wst[:, at[0], 2, k, :],
                                        start=(k == 0), stop=(k == KT - 1))
                ins.then_inc(job_ready[bank_of(key)], 1)

            def den_job(seg, t):
                bank = bank_free(("den", t), seg)
                s = Seg(t, seg.i)
                pe.wait_ge(sum_a, s.count(ST - 1, ST - 1))
                pe.wait_ge(sum_b, s.count(ST - 1, ST - 1))
                for h in range(2):
                    ins = pe.matmul(bank[DH * h:DH * h + DH, :], ones[:, 0:DH], acc[:, t % 2, h, :], start=True, stop=True)
                ins.then_inc(job_ready[bank_of(("den", t))], 1)

            def y_job(seg, t, half):
                key = ("y", t, half)
                bank = bank_free(key, seg)
                s = Seg(t, seg.i)
                pe.wait_ge(norm_done, s.count(1, 1))
                p = t // NBS
                pe.wait_ge(wo_scaled, p + 1 if seg.i is None else p + 1 + 2 * seg.i)
                for m in range(2):
                    n0 = P * (2 * half + m)
                    ins = pe.matmul(bank[:, DM * m:DM * m + DM], oT[:, t % 2, n0:n0 + P], wo_g[:, p % 2, :], start=True, stop=True)
                ins.then_inc(job_ready[bank_of(key)], 1)

            def loaded(p, seg):
                v = 64 * (p // 2 + 1)
                return p % 2, v if seg is None or seg.i is None else v + 64 * seg.i

            def scores(seg, st):
                t0, r = seg.t0, rows_of(st)
                g, p = ST * t0 + st, t0 // NBS
                if st == 0:
                    keys = [("k", p, b) for b in range(SB)] if t0 % NBS == 0 and t0 else []
                    await_all_taken(pe, keys + [("q", t0)], seg)
                if t0 == 0 and st % 4 == 0:
                    await_taken(pe, ("k", 0, st // 4))
                if g >= 2:
                    pe.wait_ge(exp_done, seg.count(ST, st - 1))
                for h in range(2):
                    for part in range(2):
                        ins = pe.matmul(sc[0:r, g % 2, h, :], kb[p % 2][:, h, part, P * st:P * st + r], qb[:, t0 % 2, h, :],
                                        start=(part == 0), stop=(part == 1))
                ins.then_inc(scores_ready, 1)

            def values(seg, st):
                t0, r = seg.t0, rows_of(st)
                g, p = ST * t0 + st, t0 // NBS
                if st % 4 == 0 and t0 % NBS == 0:
                    await_taken(pe, ("v", p, st // 4), seg)
                if st == 0 and t0 >= 2:
                    pe.wait_ge(norm_done, seg.count(1, -1))
                pe.wait_ge(clip_done, seg.count(ST, st + 1))
                for h in range(2):
                    ins = pe.matmul(ps_o[DH * h:DH * h + DH, t0 % 2, :], vb[0:r, p % 2, st, DH * h:DH * h + DH],
                                    e_buf[0:r, g % E_BUFS, h, :], start=(st == 0), stop=(st == ST - 1))
                ins.then_inc(pv_done, 1)

            pe.wait_ge(ident_done, 1)
            pe.wait_ge(const_done, 1)
            for b in range(SB):
                tiles = range(4 * b, min(4 * b + 4, ST))
                pe.wait_ge(ctx_norm, tiles[-1] + 1)
                for k in range(KT):
                    transposes(("cT", b, k), [(rows_of(t), crow[0:rows_of(t), t, P * k:P * k + P]) for t in tiles])

            def lat_transpose(b, k):
                pe.wait_ge(lat_norm, 4 * b + 4)
                transposes(("lT", b, k), [(P, z[:, 4 * b + i, P * k:P * k + P]) for i in range(4)])

            for k in range(KT):
                lat_transpose(0, k)
            q_job(None, 0, loaded(0, None))
            for k in range(KT):
                await_taken(pe, ("cT", SB - 1, k))
            for b in range(SB):
                k_job(None, 0, b, loaded(0, None))
            scores(Seg(0), 0)
            scores(Seg(0), 1)
            for b in range(SB):
                v_job(None, 0, b, loaded(0, None))

            def w_transposes(key):
                _, m, j = key
                pe.wait_ge(w_quant, 2 * m + 2)
                tiles = []
                for n in range(4 * j, 4 * j + 4):
                    if m < 2:
                        k, f = n // FT, n % FT
                        at = DM * (FT * m + f) + P * k
                        tiles.append((P, zf[:, at:at + P]))
                    else:
                        f, d = n // KT, n % KT
                        tiles.append((P, wpiece[4 + d][:, P * f:P * f + P]))
                transposes(key, tiles)

            def run(seg):
                t0 = seg.t0
                for st in range(ST):
                    if st + 2 < ST:
                        scores(seg, st + 2)
                    elif t0 + 1 < SEGS:
                        scores(seg.next(), st + 2 - ST)
                    for key in [k for at, k in segment_jobs(t0) if at == st]:
                        kind = key[0]
                        if kind == "den":
                            den_job(seg, t0 - 1)
                        elif kind == "q":
                            q_job(seg, t0 + 1, loaded((t0 + 1) // NBS, seg))
                        elif kind == "k":
                            k_job(seg, key[1], key[2], loaded(key[1], seg))
                        elif kind == "v":
                            v_job(seg, key[1], key[2], loaded(key[1], seg))
                        elif kind == "y":
                            y_job(seg, t0 - 1, key[2])
                        elif kind == "lT":
                            lat_transpose(key[1], key[2])
                        else:
                            w_transposes(key)
                    values(seg, st)

            segments(pe, run)
            end = Seg(SEGS)
            den_job(end, SEGS - 1)
            y_job(end, SEGS - 1, 0)
            y_job(end, SEGS - 1, 1)

            def spread_max(n):
                if n:
                    pe.wait_ge(scale_done, n)
                pe.wait_ge(col_ready, n + 1)
                pe.transpose(ps[0:1, 7, 0:P], fsc[:, n, 0:1], ident[:, :]).then_inc(colT_ready, 1)

            def spread_scale(n):
                pe.wait_ge(max_ready, n + 1)
                pe.matmul(ps[:, 7, 0:2], ones[0:1, :], frow[:, n, 2:4], start=True, stop=True).then_inc(bc_ready, 1)

            def split(out_ap, lhs, rhs, first, last):
                for n, (i, j) in enumerate(((0, 0), (0, 1), (1, 0))):
                    ins = pe.matmul(out_ap, lhs(i), rhs(j), start=(first and n == 0), stop=(last and n == 2))
                return ins

            await_taken(pe, ("y", SEGS - 1, 0))
            await_taken(pe, ("y", SEGS - 1, 1))
            pe.wait_ge(exp_done, ST * SEGS)
            for j in range(KT * NBS):
                k, b = j % KT, j // KT
                if j == KT * NBS - 1:
                    spread_max(0)
                    spread_scale(0)
                    pe.wait_ge(scale_done, 1)
                pe.wait_ge(h_norm, 4 * b + 4)
                for i in range(4):
                    ins = pe.transpose(ps[:, j, P * i:P * i + P], z[:, 4 * b + i, P * k:P * k + P], ident[:, :])
                ins.then_inc(hT_ready, 1)
            half = FT * NBS
            for c in range(2 * half):
                m, f, b = c // half, c // NBS % FT, c % NBS
                if c < NBS:
                    pe.wait_ge(h_low, KT * b + KT)
                if c < 7:
                    pe.wait_ge(h_int, c + 1)
                else:
                    pe.wait_ge(f1_out, c - 6)
                for k in range(KT):
                    ins = split(ps[:, c % 7, :], lambda i: wgu[:, m, i, k, P * f:P * f + P],
                                lambda j: hT[:, j, k, b * NB:(b + 1) * NB], k == 0, k == KT - 1)
                ins.then_inc(f1_ready, 1)
                if c == half + 1:
                    spread_max(1)
                if c == half + 2:
                    spread_scale(1)
            for n in (2, 3, 4):
                spread_max(n)
                spread_scale(n)
            for g in range(NT // 2):
                pe.wait_ge(o_low, g + 1)
                if g >= 4:
                    pe.wait_ge(f2_out, g - 3)
                for m in range(2):
                    for f in range(FT):
                        ins = split(ps[:, g % 4, DM * m:DM * m + DM], lambda i: ohl[:, g % 2, i, f, P * m:P * m + P],
                                    lambda j: wdT[:, j, f, :], f == 0, f == FT - 1)
                ins.then_inc(f2_ready, 1)


_INS = ['x', 'ctx_1024', 'g_xattn', 'g_ffn', 'L0_xattn_ln_l_w', 'L0_xattn_ln_l_b', 'L0_xattn_ln_c_w', 'L0_xattn_ln_c_b',
        'L0_xattn_Wq', 'L0_xattn_Wkv', 'L0_xattn_Wo', 'L0_xattn_bo', 'L0_ffn_w_gate', 'L0_ffn_w_up', 'L0_ffn_w_down']


def kernel(**inputs):
    import numpy as _np
    import concourse.bacc as _bacc
    from concourse import mybir as _mybir
    from concourse.bass_utils import run_bass_kernel_spmd as _run

    nc = _bacc.Bacc("TRN2", target_bir_lowering=False, num_devices=1)
    arrays, args = {}, []
    for name in _INS:
        a = _np.ascontiguousarray(inputs[name])
        arrays[f"in_{name}_dram"] = a
        args.append(nc.dram_tensor(f"in_{name}_dram", a.shape, _mybir.dt.from_np(a.dtype), kind="ExternalInput").ap())
    args.append(nc.dram_tensor("out_0_dram", (1, N, DM), F32, kind="ExternalOutput").ap())
    attention_ffn(nc, *args)
    r = _run(nc, [arrays], core_ids=[0])
    return r.results[0]["out_0_dram"]
```

```python
from contextlib import ExitStack

import concourse.bass as bass
from concourse import mybir

ALU = mybir.AluOpType
ACT = mybir.ActivationFunctionType
AX_X = mybir.AxisListType.X
F32 = mybir.dt.float32
F32R = mybir.dt.float32r
I16 = mybir.dt.int16
I32 = mybir.dt.int32
U16T = mybir.dt.uint16

P = 128
N, S, DM = 2048, 1601, 256
H, DH = 16, 64
FF = 768
QB = 32
KT = DM // P
PAIRS = H // 2
NB = 512
NBS = N // NB
NT = N // P
ST = -(-S // P)
SLAST = S - (ST - 1) * P
SB = -(-S // NB)
LN3 = ST + NT
SEGS = PAIRS * NBS
LOOP0, LOOPS, UNROLL = 1, 3, 8
TAIL0 = LOOP0 + LOOPS * UNROLL
WQ0, WT0 = TAIL0, SEGS - NBS
E_BUFS = 4
EPS = 1e-5
CLIP = 11.0
EXP_LO, EXP_HI = 1.6701700790245659e-05, 59874.14171519782
MAGIC = 12582912.0
QMAX = 32767.0
ROOT_MAGIC = 1597463007.0
NEWTON = 3
WMAX = 7.0
U16 = 65536.0
FT = FF // P
WBLK = FF // QB
FC = 2 * NB
FCH = FT * N // FC


def rows_of(st):
    return P if st < ST - 1 else SLAST


def cols_of(b):
    return min(NB, S - b * NB)


class Seg:

    def __init__(self, t0, i=None):
        self.t0, self.i = t0, i

    def count(self, per_segment, c):
        v = per_segment * self.t0 + c
        return v if self.i is None else v + per_segment * UNROLL * self.i

    def next(self):
        return Seg(self.t0 + 1, self.i)


def segment_jobs(t):
    if t == 0:
        return [(2, ("lT", 1, 0)), (2, ("lT", 1, 1)), (4, ("q", 1)), (5, ("lT", 2, 0)), (6, ("lT", 2, 1)),
                (7, ("k", 1, 0)), (9, ("lT", 3, 0)), (10, ("lT", 3, 1)), (11, ("v", 1, 0))]
    jobs = [(1, ("den", t - 1))]
    if t == SEGS - 1:
        return jobs + [(6, ("y", t - 1, 0)), (7, ("y", t - 1, 1))]
    if t + 1 < SEGS:
        jobs.append((3, ("q", t + 1)))
    p = t // NBS + 1
    wm = t - WT0
    if p < PAIRS:
        jobs.append((6, ("k", p, t % NBS)))
    elif wm < 3:
        jobs += [(6, ("wT", wm, 0)), (8, ("wT", wm, 1))]
    jobs += [(8, ("y", t - 1, 0)), (10, ("y", t - 1, 1))] if p < PAIRS else [(9, ("y", t - 1, 0)), (11, ("y", t - 1, 1))]
    if p < PAIRS:
        jobs.append((11, ("v", p, t % NBS)))
    elif wm < 3:
        jobs.append((12, ("wT", wm, 2)))
    return jobs


def job_table():
    order = [("cT", b, k) for b in range(SB) for k in range(KT)]
    order += [("lT", 0, k) for k in range(KT)] + [("q", 0)]
    order += [("k", 0, b) for b in range(SB)] + [("v", 0, b) for b in range(SB)]
    for t in range(SEGS):
        order += [key for _, key in segment_jobs(t)]
    order += [("den", SEGS - 1), ("y", SEGS - 1, 0), ("y", SEGS - 1, 1)]
    return {key: n for n, key in enumerate(order)}


JOBS = job_table()
PER_LOOP = 6 * UNROLL // 2


def bank_of(key):
    return JOBS[key] % 2


def place_of(key, seg):
    n = JOBS[key] // 2
    return n if seg is None or seg.i is None else n + PER_LOOP * seg.i


def attention_ffn(nc, x, ctx_rows, g_xattn, g_ffn, ln_l_w, ln_l_b, ln_c_w, ln_c_b,
                  Wq, Wkv, Wo, bo, w_gate, w_up, w_down, out):
    with ExitStack() as ctx:
        def sb(name, shape, dt=F32, stack=ctx):
            return stack.enter_context(nc.sbuf_tensor(name, shape, dt))

        def sem(name):
            return ctx.enter_context(nc.semaphore(name))

        xacc = sb("xacc", [P, NT, DM])
        z = sb("z", [P, NT, DM])
        ident = sb("ident", [P, P])
        ones = sb("ones", [P, P])
        gates = sb("gates", [P, 2])
        tg = sb("tg", [P, 2])
        cols = sb("cols", [P, 4, KT])
        bo_t = sb("bo_t", [P, DM])
        stats = sb("stats", [P, LN3 + NT, 6])
        mv = sb("mv", [P, LN3 + NT, 2])
        lnt = sb("lnt", [P, 4, LN3 + NT])
        fst = sb("fst", [P, 5, 32])
        wdT = sb("wdT", [P, 2, FT, DM], F32R)
        with ExitStack() as early:
            ctxT = sb("ctxT", [P, KT, S], stack=early)
        wgu = sb("wgu", [P, 2, 2, KT, FF], F32R)

        with ExitStack() as att:
            latT = sb("latT", [P, KT, N], stack=att)
            vb = sb("vb", [P, 2, ST, P], stack=att)
            qb = sb("qb", [P, 2, 2, 2, NB], F32R, stack=att)
            kb = [sb(name, [P, 2, S], F32R, stack=att) for name in ("kb_even", "kb_odd")]
            e_buf = sb("e_buf", [P, E_BUFS, 2, NB], stack=att)
            acc = sb("acc", [P, 2, 2, NB], stack=att)
            rden = sb("rden", [P, NB], stack=att)
            oT = sb("oT", [P, 2, NB], stack=att)
            wst = sb("wst", [P, 2, 3, KT, P], stack=att)
            wo_raw = sb("wo_raw", [P, 2, DM], stack=att)
            wo_g = sb("wo_g", [P, 2, DM], stack=att)
            wdown1 = sb("wdown1", [P, FF], stack=att)
            wsc = sb("wsc", [P, 6, 3, WBLK], stack=att)
            e_flat = e_buf[:, :, :, :].rearrange("p a b n -> p (a b n)")
            crow = e_flat[:, 0:ST * DM].rearrange("p (t d) -> p t d", d=DM)

        with ExitStack() as ffn:
            fsc = sb("fsc", [P, 5, 4], stack=ffn)
            frow = sb("frow", [1, 5, 4], stack=ffn)
            pre = sb("pre", [1, 5], stack=ffn)
            gt = sb("gt", [P, FT, N], stack=ffn)
            with ExitStack() as first:
                hT = sb("hT", [P, 2, KT, N], F32R, stack=first)
                up = sb("up", [P, FT, N], stack=first)
            ui = sb("ui", [P, FT, N], I16, stack=ffn)
            sb("pad2", [P, (2 * KT * N - FT * N // 2)], stack=ffn)
            ohl = sb("ohl", [P, 2, 2, FT, DM], F32R, stack=ffn)
            oi = sb("oi", [P, 2, FT, DM], I16, stack=ffn)
        zf = z[:, :, :].rearrange("p t d -> p (t d)")
        hi16 = zf[:, 0:N].bitcast(I16)
        sg = zf[:, 0:2 * FC].rearrange("p (a f n) -> p a f n", a=2, f=2)
        gi = zf[:, 2 * FC:3 * FC].bitcast(I16).rearrange("p (a f n) -> p a f n", a=2, f=2)
        su = zf[:, 3 * FC:4 * FC].bitcast(U16T).rearrange("p (a f n) -> p a f n", a=2, f=2)
        wpiece = [zf[:, FF * n:FF * n + FF] for n in range(5)] + [wdown1[:, :]]

        psum = nc.psum_tensor("ps", [P, 8, NB], F32)
        ps = ctx.enter_context(psum)
        ps_s, ps_o, ps_m = ps[:, 0:4, :], ps[:, 4:6, :], ps[:, 6:8, :]
        sc = ps_s.rearrange("p (a h) n -> p a h n", h=2)

        in_ctx, in_x = [sem(f"in_ctx{b}") for b in range(SB)], [sem(f"in_x{b}") for b in range(NBS)]
        in_small, in_w = sem("in_small"), sem("in_w")
        w_loaded = [sem("w_loaded0"), sem("w_loaded1")]
        ident_zero, ident_done = sem("ident_zero"), sem("ident_done")
        dve_chain = sem("dve_chain")
        ctx_norm, lat_norm, lat_root, lat_pool = sem("ctx_norm"), sem("lat_norm"), sem("lat_root"), sem("lat_pool")
        w_inverse, w_scaled, w_round, w_quant = sem("w_inverse"), sem("w_scaled"), sem("w_round"), sem("w_quant")
        tanh_done, wo_scaled, bias_added, bias_scaled = sem("tanh_done"), sem("wo_scaled"), sem("bias_added"), sem("bias_scaled")
        job_ready = [sem("job_ready0"), sem("job_ready1")]
        job_taken = [sem("job_taken0"), sem("job_taken1")]
        q_high, k_high, w_high = sem("q_high"), sem("k_high"), sem("w_high")
        scores_ready, exp_done, clip_done, pv_done = sem("scores_ready"), sem("exp_done"), sem("clip_done"), sem("pv_done")
        sum_a, sum_b = sem("sum_a"), sem("sum_b")
        norm_done, last_norm = sem("norm_done"), sem("last_norm")
        h_norm, h_top, hT_ready, h_int_a, h_int_v, h_high, h_low = sem("h_norm"), sem("h_top"), sem("hT_ready"), sem("h_int_a"), sem("h_int_v"), sem("h_high"), sem("h_low")
        col_ready, colT_ready, max_ready, bc_ready = sem("col_ready"), sem("colT_ready"), sem("max_ready"), sem("bc_ready")
        scale_done = sem("scale_done")
        f1_ready, f1_out = sem("f1_ready"), sem("f1_out")
        gi_done, sig_done, su_done = sem("gi_done"), sem("sig_done"), sem("su_done")
        gs_done, gq_done, ui_done, ui_pool, o_done = sem("gs_done"), sem("gq_done"), sem("ui_done"), sem("ui_pool"), sem("o_done")
        oi_done, o_high, o_low = sem("oi_done"), sem("o_high"), sem("o_low")
        f2_ready, f2_out, stored = sem("f2_ready"), sem("f2_out"), sem("stored")

        block = ctx.enter_context(nc.Block())

        def await_job(eng, key, seg=None):
            eng.wait_ge(job_ready[bank_of(key)], place_of(key, seg) + 1)

        def await_taken(eng, key, seg=None):
            eng.wait_ge(job_taken[bank_of(key)], place_of(key, seg) + 1)

        def await_all_taken(eng, keys, seg=None):
            for bank in range(2):
                mine = [key for key in keys if bank_of(key) == bank]
                if mine:
                    await_taken(eng, max(mine, key=JOBS.get), seg)

        def segments(eng, run):
            run(Seg(0))
            with eng.Fori(0, LOOPS) as i:
                for t0 in range(LOOP0, LOOP0 + UNROLL):
                    run(Seg(t0, i))
            for t in range(TAIL0, SEGS):
                run(Seg(t))

        def chunk(a, e):
            f, b = 2 * (e // NBS), e % NBS
            return a[:, f:f + 2, b * NB:(b + 1) * NB]

        def h_piece(j):
            return hi16[:, j * NB:(j + 1) * NB]

        def f1_place(c):
            m, c = divmod(c, FT * NBS)
            return m, c // (2 * NBS) * 2 + c % 2, c // 2 % NBS

        def w_at(m, part, j):
            if m == 2:
                return wdT[:, part, :, :].rearrange("p f d -> p (f d)")[:, j * NB:(j + 1) * NB]
            return wgu[:, m, part, :, :].rearrange("p k f -> p (k f)")[:, j * NB:(j + 1) * NB]

        def await_ui(eng, e):
            eng.wait_ge((ui_pool, ui_done)[e % 2], e // 2 + 1)

        @block.sync
        def _(sp):
            for b in range(SB - 1):
                sp.dma_start(crow[:, 4 * b:4 * b + 4, :],
                             ctx_rows[0, b * NB:(b + 1) * NB, :].rearrange("(t p) d -> p t d", p=P)).then_inc(in_ctx[b], 16)
            sp.dma_start(crow[0:SLAST, ST - 1, :], ctx_rows[0, (ST - 1) * P:S, :]).then_inc(in_ctx[SB - 1], 16)

            def load_x(b):
                sp.dma_start(xacc[:, 4 * b:4 * b + 4, :],
                             x[0, b * NB:(b + 1) * NB, :].rearrange("(t p) d -> p t d", p=P)).then_inc(in_x[b], 16)

            load_x(0)
            for n, a in enumerate((ln_l_w, ln_l_b, ln_c_w, ln_c_b)):
                sp.dma_start(cols[:, n, :], a.rearrange("(k p) -> p k", k=KT), allow_slow_non_contiguous=True).then_inc(in_small, 16)
            for n, a in enumerate((g_xattn, g_ffn)):
                sp.dma_start(gates[:, n:n + 1], a.rearrange("(a n) -> a n", a=1).to_broadcast([P, 1])).then_inc(in_small, 16)
            sp.dma_start(bo_t[:, :], bo.rearrange("(a n) -> a n", a=1).to_broadcast([P, DM])).then_inc(in_small, 16)

            def load_pair(p, parity):
                for n, (w, at) in enumerate(((Wq, 0), (Wkv, 0), (Wkv, H * DH))):
                    sp.dma_start(wst[:, parity, n, :, :],
                                 w[:, bass.ds(P * p + at, P)].rearrange("(k q) n -> q k n", q=P)).then_inc(w_loaded[parity], 16)
                sp.dma_start(wo_raw[:, parity, :], Wo[bass.ds(P * p, P), :]).then_inc(w_loaded[parity], 16)

            load_pair(0, 0)
            for b in range(1, NBS):
                load_x(b)
            load_pair(1, 1)

            def run(seg):
                if seg.t0 % NBS != NBS - 1 or (seg.t0 + 5) // NBS >= PAIRS:
                    return
                p = (seg.t0 + 5) // NBS
                await_taken(sp, ("q", seg.t0), seg)
                sp.wait_ge(wo_scaled, p - 1 if seg.i is None else p - 1 + 2 * seg.i)
                load_pair(p if seg.i is None else p + 2 * seg.i, p % 2)

            segments(sp, run)
            await_taken(sp, ("lT", NBS - 1, 1))
            for n, w in enumerate((w_gate, w_up)):
                sp.dma_start(zf[:, n * FT * DM:(n + 1) * FT * DM].rearrange("p (t d) -> p t d", d=DM),
                             w.rearrange("(t p) d -> p t d", p=P)).then_inc(in_w, 16)
            for n in range(KT):
                sp.dma_start(wpiece[4 + n], w_down[P * n:P * n + P, :]).then_inc(in_w, 16)
            for g in range(NT // 2):
                sp.wait_ge(f2_out, g + 1)
                sp.dma_start(out[0, 2 * g * P:(2 * g + 2) * P, :].rearrange("(t p) d -> p t d", p=P),
                             z[:, 2 * g:2 * g + 2, :]).then_inc(stored, 16)
            sp.wait_ge(stored, 16 * (NT // 2))

        @block.gpsimd
        def _(pool):
            pool.memset(ident[:, :], 0.0).then_inc(ident_zero, 1)
            pool.wait_ge(ident_zero, 1)
            pool.affine_select(out=ident[:, :], in_=ident[:, :], compare_op=ALU.not_equal, fill=1.0, base=0,
                               pattern=[[-1, P]], channel_multiplier=1).then_inc(ident_done, 1)
            pool.wait_ge(tanh_done, 1)
            pool.wait_ge(in_small, 16 * 7)
            pool.tensor_scalar(bo_t[:, :], bo_t[:, :], tg[:, 0:1], None, ALU.mult).then_inc(bias_scaled, 1)
            pool.wait_ge(bias_scaled, 1)
            pool.wait_ge(lat_root, 1)
            for t in range(4, NT):
                n = ST + t
                pool.tensor_scalar(z[:, t, :], xacc[:, t, :], lnt[:, 1, n:n + 1], lnt[:, 3, n:n + 1],
                                   ALU.mult, ALU.add).then_inc(lat_pool, 1)
            pool.wait_ge(lat_norm, 4)
            pool.wait_ge(lat_pool, NT - 4)

            def run(seg):
                t0 = seg.t0
                if t0 % NBS == 0:
                    p = t0 // NBS
                    pool.wait_ge(w_loaded[p % 2], (p // 2 + 1) * 64 if seg.i is None else (p // 2 + 1) * 64 + 64 * seg.i)
                    if t0 > NBS:
                        await_job(pool, ("y", t0 - NBS - 1, 1), seg)
                    pool.tensor_tensor(wo_g[:, p % 2, :], wo_raw[:, p % 2, :], tg[:, 0:1].to_broadcast([P, DM]),
                                       ALU.mult).then_inc(wo_scaled, 1)
                for st in range(1, ST):
                    r = rows_of(st)
                    pool.wait_ge(clip_done, seg.count(ST, st + 1))
                    if st == 1:
                        if t0 >= 2:
                            await_job(pool, ("den", t0 - 2), seg)
                        a = e_buf[:, (ST * t0) % E_BUFS, 1, :]
                    else:
                        pool.wait_ge(sum_b, seg.count(ST - 1, st - 1))
                        a = acc[0:r, t0 % 2, 1, :]
                    pool.tensor_tensor(acc[0:r, t0 % 2, 1, :], a, e_buf[0:r, (ST * t0 + st) % E_BUFS, 1, :],
                                       ALU.add).then_inc(sum_b, 1)
                    if t0 == 0 and st > ST - 9:
                        for t in range(2 * (st - ST + 8), 2 * (st - ST + 9)):
                            pool.tensor_tensor(xacc[:, t, :], xacc[:, t, :], bo_t[:, :], ALU.add).then_inc(bias_added, 1)

                    n, at = divmod(st, 6)
                    if WQ0 <= t0 < WT0 and at in (2, 5) and n < 2:
                        w = 2 * (t0 - WQ0) + (0 if at == 2 else 1)
                        blocks = wpiece[w].rearrange("p (n e) -> p n e", e=QB)
                        by = wsc[:, w, 2 - n, :].unsqueeze(2).to_broadcast([P, WBLK, QB])
                        pool.wait_ge((w_inverse, w_round)[n], w + 1)
                        pool.tensor_tensor(blocks, blocks, by, ALU.mult).then_inc((w_scaled, w_quant)[n], 1)

            segments(pool, run)

            for e in range(FCH):
                pool.wait_ge(sig_done, e + 1)
                if e >= 2:
                    pool.wait_ge(gs_done, e - 1)
                pool.tensor_scalar(su[:, e % 2, :, :], sg[:, e % 2, :, :], U16, 1.0, ALU.mult, ALU.mult).then_inc(su_done, 1)
            pool.wait_ge(scale_done, 3)
            for e in range(0, FCH, 2):
                pool.tensor_scalar(chunk(ui, e), chunk(up, e), fsc[:, 2, 2:3], 1.0, ALU.mult, ALU.mult).then_inc(ui_pool, 1)

        @block.scalar
        def _(act):
            act.wait_ge(in_small, 16 * 7)
            nc.scalar.activation(tg[:, :], gates[:, :], ACT.Tanh).then_inc(tanh_done, 1)

            def take_T(key, dst, n, w):
                k = key[2]
                await_job(act, key)
                nc.scalar.activation(dst[:, k, key[1] * NB:key[1] * NB + w], ps_m[:, bank_of(key), 0:w], ACT.Identity,
                                     bias=cols[:, n + 1, k:k + 1], scale=cols[:, n, k:k + 1]).then_inc(job_taken[bank_of(key)], 1)

            def q_take(seg, t, heads):
                for h in heads:
                    await_job(act, ("q", t), seg)
                    for half in range(2):
                        nc.scalar.copy(qb[DH * half:DH * half + DH, t % 2, h, 0, :],
                                       ps_m[DH * h:DH * h + DH, bank_of(("q", t)), :]).then_inc(q_high, 1)

            def k_take(seg, p, b):
                w = cols_of(b)
                await_job(act, ("k", p, b), seg)
                for h in range(2):
                    nc.scalar.copy(kb[p % 2][0:DH, h, b * NB:b * NB + w],
                                   ps_m[DH * h:DH * h + DH, bank_of(("k", p, b)), 0:w]).then_inc(k_high, 1)

            def v_take(seg, p, b):
                key = ("v", p, b)
                await_job(act, key, seg)
                if b < SB - 1:
                    nc.scalar.copy(vb[:, p % 2, 4 * b:4 * b + 4, :],
                                   ps_m[:, bank_of(key), :].rearrange("p (t n) -> p t n", n=P)).then_inc(job_taken[bank_of(key)], 1)
                else:
                    nc.scalar.copy(vb[0:SLAST, p % 2, ST - 1, :], ps_m[0:SLAST, bank_of(key), 0:P]).then_inc(job_taken[bank_of(key)], 1)

            for b in range(SB):
                for k in range(KT):
                    take_T(("cT", b, k), ctxT, 2, cols_of(b))
            for k in range(KT):
                take_T(("lT", 0, k), latT, 0, NB)
            q_take(None, 0, (0, 1))
            for b in range(SB):
                k_take(None, 0, b)
            for b in range(SB):
                v_take(None, 0, b)

            def w_take(m, j):
                key = ("wT", m, j)
                await_job(act, key)
                nc.scalar.copy(w_at(m, 0, j), ps_m[:, bank_of(key), :]).then_inc(w_high, 1)

            def run(seg):
                t0 = seg.t0
                for st in range(ST):
                    r, g = rows_of(st), ST * t0 + st
                    act.wait_ge(scores_ready, seg.count(ST, st + 1))
                    if g >= E_BUFS:
                        act.wait_ge(pv_done, seg.count(ST, st + 1 - E_BUFS))
                        back = Seg(t0 if st >= E_BUFS else t0 - 1, seg.i)
                        s0 = max((st - E_BUFS) % ST, 1)
                        act.wait_ge(sum_a, back.count(ST - 1, s0))
                        act.wait_ge(sum_b, back.count(ST - 1, s0))
                    nc.scalar.activation(e_buf[0:r, g % E_BUFS, :, :], sc[0:r, g % 2, :, :], ACT.Exp,
                                         scale=float(DH) ** -0.5).then_inc(exp_done, 1)
                    p = t0 // NBS + 1
                    if t0 == 0:
                        for b, k in {3: [(1, 0)], 4: [(1, 1)], 7: [(2, 0)], 8: [(2, 1)], 11: [(3, 0)], 12: [(3, 1)]}.get(st, []):
                            take_T(("lT", b, k), latT, 0, NB)
                    if st in (5, 6) and t0 + 1 < SEGS:
                        q_take(seg, t0 + 1, (st - 5,))
                    if WT0 <= t0 < WT0 + 3 and st in (7, 9, 12):
                        w_take(t0 - WT0, (7, 9, 12).index(st))
                    if st == (8 if t0 == 0 else 7) and p < PAIRS:
                        k_take(seg, p, t0 % NBS)
                    if st == 12 and p < PAIRS:
                        v_take(seg, p, t0 % NBS)

            segments(act, run)

            act.wait_ge(scale_done, 1)
            for j in range(KT * NBS):
                k, b = j % KT, j // KT
                if k == 0:
                    act.wait_ge(hT_ready, max(j, 6) + 1)
                    nc.scalar.activation(h_piece(j), ps[:, j, :], ACT.Copy, scale=fsc[:, 0, 2:3]).then_inc(h_int_a, 1)
                act.wait_ge((h_int_a, h_int_v)[k], b + 1)
                nc.scalar.copy(hT[:, 0, k, b * NB:(b + 1) * NB], h_piece(j)).then_inc(h_high, 1)
            half = FT * NBS

            def f1_take(c):
                m, f, b = f1_place(c)
                act.wait_ge(f1_ready, c + 1)
                nc.scalar.copy((gt, up)[m][:, f, b * NB:(b + 1) * NB], ps[:, c % 7, :]).then_inc(f1_out, 1)

            for c in range(half):
                f1_take(c)
            for e in range(FCH):
                f1_take(half + 2 * e)
                f1_take(half + 2 * e + 1)
                if e == 0:
                    act.wait_ge(scale_done, 2)
                    act.wait_ge(h_low, KT * NBS)
                if e >= 2:
                    act.wait_ge(su_done, e - 1)
                    act.wait_ge(gs_done, e - 1)
                nc.scalar.activation(gi[:, e % 2, :, :], chunk(gt, e), ACT.Copy, scale=fsc[:, 1, 2:3]).then_inc(gi_done, 1)
                act.wait_ge(gi_done, e + 1)
                nc.scalar.activation(sg[:, e % 2, :, :], gi[:, e % 2, :, :], ACT.Sigmoid, scale=fsc[:, 1, 1:2]).then_inc(sig_done, 1)
            act.wait_ge(scale_done, 3)
            for e in range(FCH):
                if e >= 2:
                    act.wait_ge(o_done, e - 1)
                nc.scalar.activation(gi[:, e % 2, :, :], chunk(gt, e), ACT.Copy, scale=fsc[:, 3, 2:3]).then_inc(gq_done, 1)
                if e % 2:
                    nc.scalar.activation(chunk(ui, e), chunk(up, e), ACT.Copy, scale=fsc[:, 2, 2:3]).then_inc(ui_done, 1)
            for g in range(NT // 2):
                act.wait_ge(oi_done, g + 1)
                if g >= 2:
                    act.wait_ge(f2_ready, g - 1)
                nc.scalar.copy(ohl[:, g % 2, 0, :, :], oi[:, g % 2, :, :]).then_inc(o_high, 1)

        @block.vector
        def _(dve):
            chain = [0]

            def link(ins):
                chain[0] += 1
                ins.then_inc(dve_chain, 1)
                dve.wait_ge(dve_chain, chain[0])

            def moments(at, src, ready=None):
                for n, a in enumerate(src):
                    if ready and n in ready:
                        dve.wait_ge(ready[n], 16)
                    ins = dve.bn_stats(stats[0:a.shape[0], at + n, :], a)
                link(ins)
                for n, a in enumerate(src):
                    ins = dve.bn_aggr(mv[0:a.shape[0], at + n, :], stats[0:a.shape[0], at + n, :])
                link(ins)

            def inverse_root(*spans):
                for first, end, c1, c0 in spans:
                    ins = dve.tensor_scalar(lnt[:, 0, first:end], mv[:, first:end, 1], c1, c0, ALU.mult, ALU.add)
                link(ins)
                a, y, u = (lnt[:, j, spans[0][0]:spans[-1][1]] for j in range(3))
                link(dve.tensor_scalar(y.bitcast(I32), a.bitcast(I32), 1, None, ALU.logical_shift_right))
                link(dve.tensor_scalar(y.bitcast(I32), y.bitcast(I32), -1.0, ROOT_MAGIC, ALU.mult, ALU.add))
                for _ in range(NEWTON):
                    link(dve.tensor_tensor(u, y, y, ALU.mult))
                    link(dve.scalar_tensor_tensor(out=u, in0=u, scalar=-0.5, in1=a, op0=ALU.mult, op1=ALU.mult))
                    link(dve.scalar_tensor_tensor(out=y, in0=u, scalar=1.5, in1=y, op0=ALU.add, op1=ALU.mult))

            def normalise(at, src, dst, done):
                for n, (a, b) in enumerate(zip(src, dst)):
                    r = a.shape[0]
                    dve.tensor_scalar(b, a, mv[0:r, at + n, 0:1], lnt[0:r, 1, at + n:at + n + 1],
                                      ALU.subtract, ALU.mult).then_inc(done, 1)

            def top(dst, src):
                return dve.tensor_reduce(dst, src, AX_X, ALU.max, apply_absolute_value=True)

            def ffn_norm(b, piece):
                at = LN3 + 4 * b
                rows = [xacc[:, t, :] for t in range(4 * b, 4 * b + 4)]
                if piece == 0:
                    moments(at, rows)
                elif piece == 1:
                    inverse_root((at, at + 4, 1.0, EPS))
                elif piece == 2:
                    normalise(at, rows, [z[:, t, :] for t in range(4 * b, 4 * b + 4)], h_norm)
                else:
                    dve.wait_ge(h_norm, 4 * b + 4)
                    top(fst[:, 0, 2 * b:2 * b + 2], z[:, 4 * b:4 * b + 4, :].rearrange("p (a t) d -> p a (t d)", a=2)).then_inc(h_top, 1)

            link(dve.memset(ones[:, :], 1.0))
            link(dve.memset(mv[:, ST - 1, :], 1.0))
            crows = [crow[0:rows_of(t), t, :] for t in range(ST)]
            lrows = [xacc[:, t, :] for t in range(NT)]
            waits = {4 * b: in_ctx[b] for b in range(SB)}
            waits[ST] = in_x[0]
            moments(0, crows + lrows[0:4], waits)
            twice = (1.0 + EPS, EPS * EPS)
            inverse_root((0, ST, 1.0, EPS), (ST, ST + 4, *twice))
            normalise(0, crows[0:4], crows[0:4], ctx_norm)
            normalise(4, crows[4:], crows[4:], ctx_norm)
            normalise(ST, lrows[0:4], [z[:, t, :] for t in range(4)], lat_norm)
            moments(ST + 4, lrows[4:], {4 * b: in_x[b + 1] for b in range(NBS - 1)})
            inverse_root((ST + 4, LN3, *twice))
            dve.scalar_tensor_tensor(out=lnt[:, 3, ST + 4:LN3], in0=mv[:, ST + 4:LN3, 0], scalar=-1.0,
                                     in1=lnt[:, 1, ST + 4:LN3], op0=ALU.mult, op1=ALU.mult).then_inc(lat_root, 1)

            def q_low(seg, t, h):
                bank = bank_of(("q", t))
                dve.wait_ge(q_high, (seg.next().count(4, 0) if seg else 0) + 2 * h + 2)
                for half in range(2):
                    lo, hi = DH * half, DH * half + DH
                    ins = dve.tensor_tensor(qb[lo:hi, t % 2, h, 1, :], ps_m[DH * h:DH * h + DH, bank, :],
                                            qb[lo:hi, t % 2, h, 0, :].bitcast(F32), ALU.subtract)
                if h == 1:
                    ins.then_inc(job_taken[bank], 1)

            def k_low(seg, p, b):
                w, bank = cols_of(b), bank_of(("k", p, b))
                for h in range(2):
                    done = 2 * (b + (p * NBS if seg is None else seg.t0 - seg.t0 % NBS + NBS)) + h + 1
                    dve.wait_ge(k_high, done + (0 if seg is None or seg.i is None else 2 * UNROLL * seg.i))
                    ins = dve.tensor_tensor(kb[p % 2][DH:P, h, b * NB:b * NB + w], ps_m[DH * h:DH * h + DH, bank, 0:w],
                                            kb[p % 2][0:DH, h, b * NB:b * NB + w].bitcast(F32), ALU.subtract)
                ins.then_inc(job_taken[bank], 1)

            for h in range(2):
                q_low(None, 0, h)
            for b in range(SB):
                k_low(None, 0, b)

            def w_scales(w):
                blocks = wpiece[w].rearrange("p (n e) -> p n e", e=QB)
                dve.wait_ge(in_w, 64)
                link(top(wsc[:, w, 0, :], blocks))
                link(dve.tensor_scalar(wsc[:, w, 1, :], wsc[:, w, 0, :], 1.0 / WMAX, 1e-12, ALU.mult, ALU.max))
                dve.reciprocal(wsc[:, w, 2, :], wsc[:, w, 1, :]).then_inc(w_inverse, 1)

            def w_integers(w):
                dve.wait_ge(w_scaled, w + 1)
                dve.tensor_scalar(wpiece[w], wpiece[w], MAGIC, MAGIC, ALU.add, ALU.subtract).then_inc(w_round, 1)

            def w_low(m, j):
                key = ("wT", m, j)
                dve.wait_ge(w_high, 3 * m + j + 1)
                dve.tensor_tensor(w_at(m, 1, j), ps_m[:, bank_of(key), :], w_at(m, 0, j).bitcast(F32),
                                  ALU.subtract).then_inc(job_taken[bank_of(key)], 1)

            def add_a(seg, st):
                t0, r = seg.t0, rows_of(st)
                if st == 1:
                    a = e_buf[:, (ST * t0) % E_BUFS, 0, :]
                else:
                    a = acc[0:r, t0 % 2, 0, :]
                    dve.wait_ge(sum_a, seg.count(ST - 1, st - 1))
                dve.wait_ge(clip_done, seg.count(ST, st + 1))
                dve.tensor_tensor(acc[0:r, t0 % 2, 0, :], a, e_buf[0:r, (ST * t0 + st) % E_BUFS, 0, :],
                                  ALU.add).then_inc(sum_a, 1)

            def invert(seg, t, c):
                bank, w = bank_of(("den", t)), NB // 4
                await_job(dve, ("den", t), seg)
                ins = dve.reciprocal(rden[:, c * w:(c + 1) * w], ps_m[:, bank, c * w:(c + 1) * w])
                if c == 3:
                    ins.then_inc(job_taken[bank], 1)

            def scale_out(seg, t):
                await_taken(dve, ("den", t), seg)
                dve.wait_ge(pv_done, Seg(t, seg.i).count(ST, ST))
                dve.tensor_tensor(oT[:, t % 2, :], ps_o[:, t % 2, :], rden[:, :], ALU.mult).then_inc(norm_done, 1)

            def add_y(seg, t, half):
                key = ("y", t, half)
                n0 = 4 * (t % NBS) + 2 * half
                await_job(dve, key, seg)
                if seg.t0 <= 4:
                    dve.wait_ge(bias_added, NT)
                dst = xacc[:, n0:n0 + 2, :]
                dve.tensor_tensor(dst, ps_m[:, bank_of(key), :].rearrange("p (t d) -> p t d", d=DM), dst,
                                  ALU.add).then_inc(job_taken[bank_of(key)], 1)

            def run(seg):
                t0 = seg.t0
                p = t0 // NBS + 1
                for st in range(ST):
                    r, g = rows_of(st), ST * t0 + st
                    dve.wait_ge(exp_done, seg.count(ST, st + 1))
                    tile = e_buf[0:r, g % E_BUFS, :, :]
                    dve.tensor_scalar(tile, tile, EXP_LO, EXP_HI, ALU.max, ALU.min).then_inc(clip_done, 1)
                    if st >= 2:
                        add_a(seg, st - 1)
                    elif st == 0 and t0 >= 1:
                        add_a(Seg(t0 - 1, seg.i), ST - 1)
                    last = t0 == SEGS - 1
                    for c in ((), range(4))[t0 >= 1]:
                        if st == (2 + c // 2 if last else 3 + c):
                            invert(seg, t0 - 1, c)
                    if st == (4 if last else 7) and t0 >= 1:
                        scale_out(seg, t0 - 1)
                    if st in (6, 7) and t0 + 1 < SEGS:
                        q_low(seg, t0 + 1, st - 6)
                    if st == (9 if t0 == 0 else 8) and p < PAIRS:
                        k_low(seg, p, t0 % NBS)
                    if WQ0 <= t0 < WT0:
                        w = 2 * (t0 - WQ0)
                        if st < 2:
                            w_scales(w + st)
                        if st in (7, 11):
                            w_integers(w + st // 11)
                    if WT0 <= t0 < WT0 + 3 and st in (8, 10):
                        w_low(t0 - WT0, st // 10)
                    if st == (7 if last else 10) and t0 >= 1:
                        add_y(seg, t0 - 1, 0)
                    if st == (8 if last else 12) and t0 >= 1:
                        add_y(seg, t0 - 1, 1)
                    if WT0 <= t0 < WT0 + 3 and st == 12:
                        w_low(t0 - WT0, 2)
                    for first, b in {SEGS - 2: [(0, 0)], SEGS - 1: [(4, 1), (9, 2)]}.get(t0, []):
                        if st == first:
                            for half in range(2):
                                await_taken(dve, ("y", SEGS - NBS + b, half))
                        if first <= st < first + 4:
                            ffn_norm(b, st - first)

            segments(dve, run)
            end = Seg(SEGS)
            add_a(Seg(SEGS - 1), ST - 1)
            t = SEGS - 1
            den_bank, w = bank_of(("den", t)), NB // 2
            await_job(dve, ("den", t))
            dve.wait_ge(pv_done, ST * SEGS)
            for half in range(2):
                part = slice(w * half, w * half + w)
                ins = dve.reciprocal(rden[:, part], ps_m[:, den_bank, part])
                if half == 0:
                    link(ins)
                else:
                    ins.then_inc(job_taken[den_bank], 1)
                    await_taken(dve, ("den", t))
                dve.tensor_tensor(oT[:, t % 2, part], ps_o[:, t % 2, part], rden[:, part], ALU.mult).then_inc(last_norm, 1)
            for half in range(2):
                add_y(end, t, half)
                await_taken(dve, ("y", t, half))
                n = NT - 4 + 2 * half
                moments(LN3 + n, [xacc[:, n, :], xacc[:, n + 1, :]])
            for piece in (1, 2, 3):
                ffn_norm(NBS - 1, piece)

            def scale_of(n, w, pieces, turn):
                top(fsc[:, n:n + w, 0], fst[:, n:n + w, 0:pieces]).then_inc(col_ready, 1)
                dve.wait_ge(colT_ready, turn + 1)
                real, row = pre[:, n:n + w], [frow[:, n:n + w, j] for j in range(4)]
                link(top(row[0], ps[0:1, 7, 0:P * w].rearrange("p (w q) -> p w q", q=P)))
                link(dve.scalar_tensor_tensor(out=row[1], in0=row[0], scalar=1.0 / QMAX, in1=real, op0=ALU.mult, op1=ALU.mult))
                link(dve.tensor_scalar(row[2], row[1], 1e-12, None, ALU.max))
                link(dve.reciprocal(row[3], row[2]))
                dve.tensor_tensor(row[3], row[3], real, ALU.mult).then_inc(max_ready, 1)
                dve.wait_ge(bc_ready, turn + 1)
                dve.tensor_copy(fsc[:, n:n + w, 1:3], ps[:, 7, 0:2 * w].rearrange("p (w q) -> p w q", q=2)).then_inc(scale_done, 1)
                dve.wait_ge(scale_done, turn + 1)

            dve.memset(pre[:, :], 1.0).then_inc(h_top, 1)
            dve.wait_ge(h_top, NBS + 1)
            scale_of(0, 1, 2 * NBS, 0)
            link(dve.tensor_scalar(pre[:, 1:3], pre[:, 1:3], frow[:, 0, 2:3], None, ALU.mult))

            def h_integers(j):
                dve.wait_ge(hT_ready, max(j, 6) + 1)
                dve.tensor_scalar(h_piece(j), ps[:, j, :], fsc[:, 0, 2:3], None, ALU.mult).then_inc(h_int_v, 1)

            h_integers(1)
            for j in range(KT * NBS):
                k, b = j % KT, j // KT
                if k == 0 and b + 1 < NBS:
                    h_integers(j + 3)
                dve.wait_ge(h_high, j + 1)
                dve.tensor_tensor(hT[:, 1, k, b * NB:(b + 1) * NB], h_piece(j),
                                  hT[:, 0, k, b * NB:(b + 1) * NB].bitcast(F32), ALU.subtract).then_inc(h_low, 1)
            pieces = FT * NBS

            def f1_top(m, e):
                dve.wait_ge(f1_out, pieces * m + 2 * e + 2)
                return top(fst[:, 1 + m, 2 * e:2 * e + 2], chunk((gt, up)[m], e))

            for e in range(FCH):
                ins = f1_top(0, e)
            link(ins)
            scale_of(1, 1, pieces, 1)
            link(dve.tensor_scalar(pre[:, 3:4], frow[:, 1, 2:3], 1.0 / U16, None, ALU.mult))
            for e in range(FCH):
                up_top = f1_top(1, e)
                if e == FCH - 1:
                    link(up_top)
                dve.wait_ge(su_done, e + 1)
                dve.tensor_tensor(chunk(gt, e), gi[:, e % 2, :, :], su[:, e % 2, :, :], ALU.mult).then_inc(gs_done, 1)
                if e >= 1:
                    dve.wait_ge(gs_done, e)
                    top(fst[:, 3, 2 * e - 2:2 * e], chunk(gt, e - 1))
            dve.wait_ge(gs_done, FCH)
            link(top(fst[:, 3, pieces - 2:pieces], chunk(gt, FCH - 1)))
            scale_of(2, 2, pieces, 2)
            link(dve.tensor_tensor(pre[:, 4:5], frow[:, 3, 2:3], frow[:, 2, 2:3], ALU.mult))
            for e in range(FCH):
                dve.wait_ge(gq_done, e + 1)
                await_ui(dve, e)
                dve.tensor_tensor(chunk(gt, e), gi[:, e % 2, :, :], chunk(ui, e), ALU.mult).then_inc(o_done, 1)
                if e >= 1:
                    dve.wait_ge(o_done, e)
                    top(fst[:, 4, 2 * e - 2:2 * e], chunk(gt, e - 1))
            dve.wait_ge(o_done, FCH)
            link(top(fst[:, 4, pieces - 2:pieces], chunk(gt, FCH - 1)))
            scale_of(4, 1, pieces, 3)
            link(dve.tensor_tensor(fsc[:, 4, 3:4], fsc[:, 4, 1:2], tg[:, 1:2], ALU.mult))

            def out_integers(g):
                if g >= 2:
                    dve.wait_ge(o_high, g - 1)
                    dve.wait_ge(o_low, g - 1)
                dve.tensor_scalar(oi[:, g % 2, :, :], gt[:, :, DM * g:DM * g + DM], fsc[:, 4, 2:3], None,
                                  ALU.mult).then_inc(oi_done, 1)

            def out_low(g):
                dve.wait_ge(o_high, g + 1)
                dve.wait_ge(oi_done, g + 1)
                dve.tensor_tensor(ohl[:, g % 2, 1, :, :], oi[:, g % 2, :, :], ohl[:, g % 2, 0, :, :].bitcast(F32),
                                  ALU.subtract).then_inc(o_low, 1)

            def result(g):
                dve.wait_ge(f2_ready, g + 1)
                dve.scalar_tensor_tensor(out=z[:, 2 * g:2 * g + 2, :], in0=ps[:, g % 4, :].rearrange("p (t d) -> p t d", d=DM),
                                         scalar=fsc[:, 4, 3:4], in1=xacc[:, 2 * g:2 * g + 2, :],
                                         op0=ALU.mult, op1=ALU.add).then_inc(f2_out, 1)

            out_integers(0)
            for g in range(NT // 2):
                if g + 1 < NT // 2:
                    out_integers(g + 1)
                out_low(g)
                if g >= 2:
                    result(g - 2)
            result(NT // 2 - 2)
            result(NT // 2 - 1)

        @block.tensor
        def _(pe):
            def bank_free(key, seg=None):
                n = place_of(key, seg)
                if JOBS[key] >= 2:
                    pe.wait_ge(job_taken[bank_of(key)], n)
                return ps_m[:, bank_of(key), :]

            def transposes(key, tiles):
                bank = bank_free(key)
                for i, (r, src) in enumerate(tiles):
                    ins = pe.transpose(bank[:, P * i:P * i + r], src, ident[0:r, 0:r])
                ins.then_inc(job_ready[bank_of(key)], 1)

            def q_job(seg, t, at):
                bank = bank_free(("q", t), seg)
                pe.wait_ge(w_loaded[at[0]], at[1])
                b = t % NBS
                if t < NBS:
                    await_all_taken(pe, [("lT", b, k) for k in range(KT)])
                for k in range(KT):
                    ins = pe.matmul(bank, wst[:, at[0], 0, k, :], latT[:, k, b * NB:(b + 1) * NB], start=(k == 0), stop=(k == KT - 1))
                ins.then_inc(job_ready[bank_of(("q", t))], 1)

            def k_job(seg, p, b, at):
                key, w = ("k", p, b), cols_of(b)
                bank = bank_free(key, seg)
                pe.wait_ge(w_loaded[at[0]], at[1])
                for k in range(KT):
                    ins = pe.matmul(bank[:, 0:w], wst[:, at[0], 1, k, :], ctxT[:, k, b * NB:b * NB + w], start=(k == 0), stop=(k == KT - 1))
                ins.then_inc(job_ready[bank_of(key)], 1)

            def v_job(seg, p, b, at):
                key = ("v", p, b)
                bank = bank_free(key, seg)
                for i, st in enumerate(range(4 * b, min(4 * b + 4, ST))):
                    r = rows_of(st)
                    for k in range(KT):
                        ins = pe.matmul(bank[0:r, P * i:P * i + P], ctxT[:, k, P * st:P * st + r], wst[:, at[0], 2, k, :],
                                        start=(k == 0), stop=(k == KT - 1))
                ins.then_inc(job_ready[bank_of(key)], 1)

            def den_job(seg, t):
                bank = bank_free(("den", t), seg)
                s = Seg(t, seg.i)
                pe.wait_ge(sum_a, s.count(ST - 1, ST - 1))
                pe.wait_ge(sum_b, s.count(ST - 1, ST - 1))
                for h in range(2):
                    ins = pe.matmul(bank[DH * h:DH * h + DH, :], ones[:, 0:DH], acc[:, t % 2, h, :], start=True, stop=True)
                ins.then_inc(job_ready[bank_of(("den", t))], 1)

            def y_job(seg, t, half):
                key = ("y", t, half)
                bank = bank_free(key, seg)
                s = Seg(t, seg.i)
                if t == SEGS - 1:
                    pe.wait_ge(last_norm, half + 1)
                else:
                    pe.wait_ge(norm_done, s.count(1, 1))
                p = t // NBS
                pe.wait_ge(wo_scaled, p + 1 if seg.i is None else p + 1 + 2 * seg.i)
                for m in range(2):
                    n0 = P * (2 * half + m)
                    ins = pe.matmul(bank[:, DM * m:DM * m + DM], oT[:, t % 2, n0:n0 + P], wo_g[:, p % 2, :], start=True, stop=True)
                ins.then_inc(job_ready[bank_of(key)], 1)

            def loaded(p, seg):
                v = 64 * (p // 2 + 1)
                return p % 2, v if seg is None or seg.i is None else v + 64 * seg.i

            def scores(seg, st):
                t0, r = seg.t0, rows_of(st)
                g, p = ST * t0 + st, t0 // NBS
                if st == 0:
                    keys = [("k", p, b) for b in range(SB)] if t0 % NBS == 0 and t0 else []
                    await_all_taken(pe, keys + [("q", t0)], seg)
                if t0 == 0 and st % 4 == 0:
                    await_taken(pe, ("k", 0, st // 4))
                if g >= 2:
                    pe.wait_ge(exp_done, seg.count(ST, st - 1))
                for h in range(2):
                    for part in range(2):
                        ins = pe.matmul(sc[0:r, g % 2, h, :], kb[p % 2][:, h, P * st:P * st + r], qb[:, t0 % 2, h, part, :],
                                        start=(part == 0), stop=(part == 1))
                ins.then_inc(scores_ready, 1)

            def values(seg, st):
                t0, r = seg.t0, rows_of(st)
                g, p = ST * t0 + st, t0 // NBS
                if st % 4 == 0 and t0 % NBS == 0:
                    await_taken(pe, ("v", p, st // 4), seg)
                if st == 0 and t0 >= 2:
                    pe.wait_ge(norm_done, seg.count(1, -1))
                pe.wait_ge(clip_done, seg.count(ST, st + 1))
                for h in range(2):
                    ins = pe.matmul(ps_o[DH * h:DH * h + DH, t0 % 2, :], vb[0:r, p % 2, st, DH * h:DH * h + DH],
                                    e_buf[0:r, g % E_BUFS, h, :], start=(st == 0), stop=(st == ST - 1))
                ins.then_inc(pv_done, 1)

            pe.wait_ge(ident_done, 1)
            for b in range(SB):
                tiles = range(4 * b, min(4 * b + 4, ST))
                pe.wait_ge(ctx_norm, tiles[-1] + 1)
                for k in range(KT):
                    transposes(("cT", b, k), [(rows_of(t), crow[0:rows_of(t), t, P * k:P * k + P]) for t in tiles])

            def lat_transpose(b, k):
                if b == 0:
                    pe.wait_ge(lat_norm, 4)
                else:
                    pe.wait_ge(lat_pool, 4 * b)
                transposes(("lT", b, k), [(P, z[:, 4 * b + i, P * k:P * k + P]) for i in range(4)])

            for k in range(KT):
                lat_transpose(0, k)
            q_job(None, 0, loaded(0, None))
            for k in range(KT):
                await_taken(pe, ("cT", SB - 1, k))
            for b in range(SB):
                k_job(None, 0, b, loaded(0, None))
            scores(Seg(0), 0)
            scores(Seg(0), 1)
            for b in range(SB):
                v_job(None, 0, b, loaded(0, None))

            def w_transposes(key):
                _, m, j = key
                pe.wait_ge(w_quant, 2 * m + 2)
                tiles = []
                for n in range(4 * j, 4 * j + 4):
                    if m < 2:
                        k, f = n // FT, n % FT
                        at = DM * (FT * m + f) + P * k
                        tiles.append((P, zf[:, at:at + P]))
                    else:
                        f, d = n // KT, n % KT
                        tiles.append((P, wpiece[4 + d][:, P * f:P * f + P]))
                transposes(key, tiles)

            def run(seg):
                t0 = seg.t0
                for st in range(ST):
                    if st + 2 < ST:
                        scores(seg, st + 2)
                    elif t0 + 1 < SEGS:
                        scores(seg.next(), st + 2 - ST)
                    for key in [k for at, k in segment_jobs(t0) if at == st]:
                        kind = key[0]
                        if kind == "den":
                            den_job(seg, t0 - 1)
                        elif kind == "q":
                            q_job(seg, t0 + 1, loaded((t0 + 1) // NBS, seg))
                        elif kind == "k":
                            k_job(seg, key[1], key[2], loaded(key[1], seg))
                        elif kind == "v":
                            v_job(seg, key[1], key[2], loaded(key[1], seg))
                        elif kind == "y":
                            y_job(seg, t0 - 1, key[2])
                        elif kind == "lT":
                            lat_transpose(key[1], key[2])
                        else:
                            w_transposes(key)
                    values(seg, st)

            segments(pe, run)
            end = Seg(SEGS)
            den_job(end, SEGS - 1)
            y_job(end, SEGS - 1, 0)
            y_job(end, SEGS - 1, 1)

            def spread_max(n, w, turn):
                if turn:
                    pe.wait_ge(scale_done, turn)
                pe.wait_ge(col_ready, turn + 1)
                for j in range(w):
                    ins = pe.transpose(ps[0:1, 7, P * j:P * j + P], fsc[:, n + j, 0:1], ident[:, :])
                ins.then_inc(colT_ready, 1)

            def spread_scale(n, w, turn):
                pe.wait_ge(max_ready, turn + 1)
                pe.matmul(ps[:, 7, 0:2 * w], ones[0:1, :], frow[:, n:n + w, 2:4], start=True, stop=True).then_inc(bc_ready, 1)

            def split(out_ap, lhs, rhs, first, last):
                for n, (i, j) in enumerate(((0, 0), (0, 1), (1, 0))):
                    ins = pe.matmul(out_ap, lhs(i), rhs(j), start=(first and n == 0), stop=(last and n == 2))
                return ins

            await_taken(pe, ("y", SEGS - 1, 0))
            await_taken(pe, ("y", SEGS - 1, 1))
            pe.wait_ge(exp_done, ST * SEGS)
            for j in range(KT * NBS):
                k, b = j % KT, j // KT
                if j == KT * NBS - 1:
                    spread_max(0, 1, 0)
                    spread_scale(0, 1, 0)
                    pe.wait_ge(scale_done, 1)
                pe.wait_ge(h_norm, 4 * b + 4)
                for i in range(4):
                    ins = pe.transpose(ps[:, j, P * i:P * i + P], z[:, 4 * b + i, P * k:P * k + P], ident[:, :])
                ins.then_inc(hT_ready, 1)
            half = FT * NBS
            for c in range(2 * half):
                m, f, b = f1_place(c)
                if c < 2 * NBS and c % 2 == 0:
                    pe.wait_ge(h_low, KT * b + KT)
                if c < 7:
                    pe.wait_ge((h_int_a, h_int_v)[c % 2], c // 2 + 1)
                else:
                    pe.wait_ge(f1_out, c - 6)
                for k in range(KT):
                    ins = split(ps[:, c % 7, :], lambda i: wgu[:, m, i, k, P * f:P * f + P],
                                lambda j: hT[:, j, k, b * NB:(b + 1) * NB], k == 0, k == KT - 1)
                ins.then_inc(f1_ready, 1)
                if c == half + 1:
                    spread_max(1, 1, 1)
                if c == half + 2:
                    spread_scale(1, 1, 1)
            for turn, n, w in ((2, 2, 2), (3, 4, 1)):
                spread_max(n, w, turn)
                spread_scale(n, w, turn)
            for g in range(NT // 2):
                pe.wait_ge(o_low, g + 1)
                if g >= 4:
                    pe.wait_ge(f2_out, g - 3)
                for m in range(2):
                    for f in range(FT):
                        ins = split(ps[:, g % 4, DM * m:DM * m + DM], lambda i: ohl[:, g % 2, i, f, P * m:P * m + P],
                                    lambda j: wdT[:, j, f, :], f == 0, f == FT - 1)
                ins.then_inc(f2_ready, 1)


_INS = ['x', 'ctx_1024', 'g_xattn', 'g_ffn', 'L0_xattn_ln_l_w', 'L0_xattn_ln_l_b', 'L0_xattn_ln_c_w', 'L0_xattn_ln_c_b',
        'L0_xattn_Wq', 'L0_xattn_Wkv', 'L0_xattn_Wo', 'L0_xattn_bo', 'L0_ffn_w_gate', 'L0_ffn_w_up', 'L0_ffn_w_down']


def kernel(**inputs):
    import numpy as _np
    import concourse.bacc as _bacc
    from concourse import mybir as _mybir
    from concourse.bass_utils import run_bass_kernel_spmd as _run

    nc = _bacc.Bacc("TRN2", target_bir_lowering=False, num_devices=1)
    arrays, args = {}, []
    for name in _INS:
        a = _np.ascontiguousarray(inputs[name])
        arrays[f"in_{name}_dram"] = a
        args.append(nc.dram_tensor(f"in_{name}_dram", a.shape, _mybir.dt.from_np(a.dtype), kind="ExternalInput").ap())
    args.append(nc.dram_tensor("out_0_dram", (1, N, DM), F32, kind="ExternalOutput").ap())
    attention_ffn(nc, *args)
    r = _run(nc, [arrays], core_ids=[0])
    return r.results[0]["out_0_dram"]
```
